# Optimizing a Trainium2 kernel written in Bass

```python
import numpy as np
import jax
import jax.numpy as jnp

def _softmax(x, axis=-1):
    return jax.nn.softmax(x, axis=axis)

def _gelu(x):
    return jax.nn.gelu(x, approximate=True)

def _silu(x):
    return jax.nn.silu(x)

def _sigmoid(x):
    return jax.nn.sigmoid(x)

def _layernorm(x, axis=-1, eps=1e-05):
    m = jnp.mean(x, axis=axis, keepdims=True)
    v = jnp.var(x, axis=axis, keepdims=True)
    return (x - m) / jnp.sqrt(v + eps)

def _scatter_add(tgt, idx, src, axis=0):
    return tgt.at[idx].add(src)

def _segment_sum(src, seg, n):
    return jax.ops.segment_sum(src, seg, n)
kernel_name = 'mk_flamingo_gated_d2_seqx_r8_40d270'

def setup_inputs(seed: int=0):
    np.random.seed(seed)
    _w = jnp.asarray

    def _rec_inputs():
        import jax
        import jax.numpy as jnp
        _rk = jax.random.key(seed)
        x = 7.22e-05 + 1 * jax.random.normal(jax.random.fold_in(_rk, 1), (8, 128, 512), jnp.float32)
        _lenS = 128 - jax.random.randint(jax.random.fold_in(_rk, 7), (8,), 0, max(1, 128 // 4) + 1, jnp.int32)
        _lenS2 = 128 - jax.random.randint(jax.random.fold_in(_rk, 8), (8,), 0, max(1, 128 // 4) + 1, jnp.int32)
        _ctx_4096P = jax.random.normal(jax.random.fold_in(_rk, 11), (8, 16, 512), jnp.float32)
        _ctx_4096c = jax.random.dirichlet(jax.random.fold_in(_rk, 511), 0.3 * jnp.ones((16,), jnp.float32), (8, 128))
        _ctx_4096t = jnp.einsum('bsk,bkd->bsd', _ctx_4096c, _ctx_4096P)
        _ctx_4096t = _ctx_4096t * jax.lax.rsqrt(jnp.mean(jnp.square(_ctx_4096t)) + 1e-12) * 0.953939
        ctx_4096 = 4.13588e-05 + 0.999923 * (_ctx_4096t + 0.3 * jax.random.normal(jax.random.fold_in(_rk, 611), (8, 128, 512), jnp.float32))
        _validS = jnp.arange(128)[None, :] < _lenS[:, None]
        _validS2 = jnp.arange(128)[None, :] < _lenS2[:, None]
        _causal = jnp.tril(jnp.ones((128, 128), dtype=bool))
        mask_BxSxS2_bk0 = jnp.logical_not(jnp.broadcast_to(_validS2[:, None, :], (8, 128, 128)))
        _g = jax.random.normal(jax.random.fold_in(_rk, 9001), (2, 2), jnp.float32)
        _g = jnp.sign(_g) * jnp.maximum(jnp.abs(_g), 1.0) + (_g == 0) * 1.0
        g_xattn = _g[0]
        g_ffn = _g[1]
        return (x, ctx_4096, mask_BxSxS2_bk0, g_xattn, g_ffn)
    x, ctx_4096, mask_BxSxS2_bk0, g_xattn, g_ffn = _rec_inputs()

    def _L0_xattn_setup():
        import jax, jax.numpy as jnp
        import numpy as np
        B, LQ, LK, D, H, DH = (2, 128, 128, 512, 32, 128)
        EPS = 1e-05

        def _rmsnorm(x, weight):
            var = jnp.mean(jnp.square(x), axis=-1, keepdims=True)
            return x * jax.lax.rsqrt(var + EPS) * weight
        key = jax.random.key(seed)
        ks = jax.random.split(key, 8)
        scale = 0.02
        return {'hidden_states': jax.random.normal(ks[0], (B, LQ, D), jnp.float32), 'key_value_states': jax.random.normal(ks[1], (B, LK, D), jnp.float32), 'attention_mask': jax.random.randint(ks[2], (B, LQ, LK), 0, 2) > 0, 'position_bias': jax.random.normal(ks[3], (H, LQ, LK), jnp.float32), 'ln_weight': jnp.ones((D,), jnp.float32), 'w_q': jax.random.normal(ks[4], (H * DH, D), jnp.float32) * scale, 'w_k': jax.random.normal(ks[5], (H * DH, D), jnp.float32) * scale, 'w_v': jax.random.normal(ks[6], (H * DH, D), jnp.float32) * scale, 'w_out': jax.random.normal(ks[7], (D, H * DH), jnp.float32) * scale}
    _L0_xattn_all = _L0_xattn_setup()
    _L0_xattn_in = {k: v for k, v in _L0_xattn_all.items() if k in ('position_bias', 'ln_weight', 'w_q', 'w_k', 'w_v', 'w_out')}
    del _L0_xattn_all

    def _L0_ffn_setup():
        import jax, jax.numpy as jnp
        import numpy as np
        B_L, B_H = (4, 8)
        LIN_SLOPE, LIN_INTER, EST_T = (1.0, 0.0, 64.0)
        BATCH, SEQ, IN_F, OUT_F = (4, 256, 512, 512)
        MAX_BITS = 8

        def dequant_kbit(qweight, lut, bit):
            O, I32 = (qweight.shape[1], qweight.shape[2])
            shifts = jnp.arange(32, dtype=jnp.int32)
            idx = jnp.zeros((O, I32 * 32), dtype=jnp.int32)
            for p in range(bit):
                bits = (qweight[p][:, :, None] >> shifts & 1).reshape(O, I32 * 32)
                idx = idx | bits << p
            return jnp.take_along_axis(lut, idx, axis=1)
        key = jax.random.key(seed)
        k = jax.random.split(key, 5)
        x = jax.random.normal(k[0], (BATCH, SEQ, IN_F), dtype=jnp.float32)
        qweight = jax.random.randint(k[1], (MAX_BITS, OUT_F, IN_F // 32), 0, 2147483647, dtype=jnp.int32)
        lut4 = jax.random.normal(k[2], (OUT_F, 2 ** B_L), dtype=jnp.float32) * 0.02
        lut8 = jax.random.normal(k[3], (OUT_F, 2 ** B_H), dtype=jnp.float32) * 0.02
        bias = jax.random.normal(k[4], (OUT_F,), dtype=jnp.float32) * 0.01
        return {'x': x, 'qweight': qweight, 'lut4': lut4, 'lut8': lut8, 'bias': bias}
    _L0_ffn_all = _L0_ffn_setup()
    _L0_ffn_in = {k: v for k, v in _L0_ffn_all.items() if k in ('qweight', 'lut4', 'lut8', 'bias')}
    del _L0_ffn_all

    def _L1_xattn_setup():
        import jax, jax.numpy as jnp
        import numpy as np
        HEADS = 32
        KV_HEADS = 8
        HEAD_DIM = 128
        EPS = 1e-06

        def rms_norm(x, w):
            var = jnp.mean(jnp.square(x.astype(jnp.float32)), axis=-1, keepdims=True)
            return (x.astype(jnp.float32) * jax.lax.rsqrt(var + EPS)).astype(x.dtype) * w
        key = jax.random.key(seed)
        ks = jax.random.split(key, 6)
        bsz, n_lat, seq, hidden = (8, 64, 512, 512)
        return {'latents': jax.random.normal(ks[0], (bsz, n_lat, hidden), jnp.float32), 'context': jax.random.normal(ks[1], (bsz, seq, hidden), jnp.float32), 'Wq': jax.random.normal(ks[2], (hidden, HEADS * HEAD_DIM), jnp.float32) * 0.02, 'Wk': jax.random.normal(ks[3], (hidden, KV_HEADS * HEAD_DIM), jnp.float32) * 0.02, 'Wv': jax.random.normal(ks[4], (hidden, KV_HEADS * HEAD_DIM), jnp.float32) * 0.02, 'Wo': jax.random.normal(ks[5], (HEADS * HEAD_DIM, hidden), jnp.float32) * 0.02, 'q_norm_w': jnp.ones((HEAD_DIM,), jnp.float32), 'k_norm_w': jnp.ones((HEAD_DIM,), jnp.float32)}
    _L1_xattn_all = _L1_xattn_setup()
    _L1_xattn_in = {k: v for k, v in _L1_xattn_all.items() if k in ('Wq', 'Wk', 'Wv', 'Wo', 'q_norm_w', 'k_norm_w')}
    del _L1_xattn_all

    def _L1_ffn_setup():
        import jax, jax.numpy as jnp
        import numpy as np
        B, S, D_IN, D_OUT = (4, 256, 512, 512)
        key = jax.random.key(seed)
        k1, k2, k3 = jax.random.split(key, 3)
        input = jax.random.normal(k1, (B, S, D_IN), dtype=jnp.float16)
        weight = jax.random.normal(k2, (D_OUT, D_IN), dtype=jnp.float16) * jnp.float16(0.02)
        bias = jax.random.normal(k3, (1, D_OUT), dtype=jnp.float16)
        return {'input': input, 'weight': weight, 'bias': bias}
    _L1_ffn_all = _L1_ffn_setup()
    _L1_ffn_in = {k: v for k, v in _L1_ffn_all.items() if k in ('weight', 'bias')}
    del _L1_ffn_all
    return {'x': x, 'ctx_4096': ctx_4096, 'mask_BxSxS2_bk0': mask_BxSxS2_bk0, 'g_xattn': g_xattn, 'g_ffn': g_ffn, 'L0_xattn_position_bias': _L0_xattn_in['position_bias'], 'L0_xattn_ln_weight': _L0_xattn_in['ln_weight'], 'L0_xattn_w_q': _L0_xattn_in['w_q'], 'L0_xattn_w_k': _L0_xattn_in['w_k'], 'L0_xattn_w_v': _L0_xattn_in['w_v'], 'L0_xattn_w_out': _L0_xattn_in['w_out'], 'L0_ffn_qweight': _L0_ffn_in['qweight'], 'L0_ffn_lut4': _L0_ffn_in['lut4'], 'L0_ffn_lut8': _L0_ffn_in['lut8'], 'L0_ffn_bias': _L0_ffn_in['bias'], 'L1_xattn_Wq': _L1_xattn_in['Wq'], 'L1_xattn_Wk': _L1_xattn_in['Wk'], 'L1_xattn_Wv': _L1_xattn_in['Wv'], 'L1_xattn_Wo': _L1_xattn_in['Wo'], 'L1_xattn_q_norm_w': _L1_xattn_in['q_norm_w'], 'L1_xattn_k_norm_w': _L1_xattn_in['k_norm_w'], 'L1_ffn_weight': _L1_ffn_in['weight'], 'L1_ffn_bias': _L1_ffn_in['bias']}

def reference(x, ctx_4096, mask_BxSxS2_bk0, g_xattn, g_ffn, L0_xattn_position_bias, L0_xattn_ln_weight, L0_xattn_w_q, L0_xattn_w_k, L0_xattn_w_v, L0_xattn_w_out, L0_ffn_qweight, L0_ffn_lut4, L0_ffn_lut8, L0_ffn_bias, L1_xattn_Wq, L1_xattn_Wk, L1_xattn_Wv, L1_xattn_Wo, L1_xattn_q_norm_w, L1_xattn_k_norm_w, L1_ffn_weight, L1_ffn_bias):
    import jax
    import jax.numpy as jnp

    def _L0_xattn_ref(hidden_states, key_value_states, attention_mask, position_bias, ln_weight, w_q, w_k, w_v, w_out):
        import jax, jax.numpy as jnp
        import numpy as np
        B, LQ, LK, D, H, DH = (2, 128, 128, 512, 32, 128)
        EPS = 1e-05

        def _rmsnorm(x, weight):
            var = jnp.mean(jnp.square(x), axis=-1, keepdims=True)
            return x * jax.lax.rsqrt(var + EPS) * weight
        x = _rmsnorm(hidden_states, ln_weight)
        b, lq, _ = x.shape
        lk = key_value_states.shape[1]
        h_q = (x @ w_q.T).reshape(b, lq, H, DH)
        h_k = (key_value_states @ w_k.T).reshape(b, lk, H, DH)
        h_v = (key_value_states @ w_v.T).reshape(b, lk, H, DH)
        score = jnp.einsum('bqhd,bkhd->bhqk', h_q, h_k)
        score = score + position_bias[None]
        m = attention_mask[:, None]
        score = jnp.where(m, score, -jnp.inf)
        score = jax.nn.softmax(score, axis=-1)
        score = jnp.where(m, score, 0.0)
        attn = jnp.einsum('bhqk,bkhd->bqhd', score, h_v).reshape(b, lq, H * DH)
        out = attn @ w_out.T
        return hidden_states + out

    def _L0_ffn_ref(x, qweight, lut4, lut8, bias):
        import jax, jax.numpy as jnp
        import numpy as np
        B_L, B_H = (4, 8)
        LIN_SLOPE, LIN_INTER, EST_T = (1.0, 0.0, 64.0)
        BATCH, SEQ, IN_F, OUT_F = (4, 256, 512, 512)
        MAX_BITS = 8

        def dequant_kbit(qweight, lut, bit):
            O, I32 = (qweight.shape[1], qweight.shape[2])
            shifts = jnp.arange(32, dtype=jnp.int32)
            idx = jnp.zeros((O, I32 * 32), dtype=jnp.int32)
            for p in range(bit):
                bits = (qweight[p][:, :, None] >> shifts & 1).reshape(O, I32 * 32)
                idx = idx | bits << p
            return jnp.take_along_axis(lut, idx, axis=1)
        e = jnp.linalg.norm(x, axis=-1) * LIN_SLOPE + LIN_INTER
        mask = e > EST_T
        w_l = dequant_kbit(qweight, lut4, B_L)
        w_h = dequant_kbit(qweight, lut8, B_H)
        y_l = jnp.einsum('bsi,oi->bso', x, w_l)
        y_h = jnp.einsum('bsi,oi->bso', x, w_h)
        y = jnp.where(mask[..., None], y_h, y_l) + bias
        return y

    def _L1_xattn_ref(latents, context, Wq, Wk, Wv, Wo, q_norm_w, k_norm_w):
        import jax, jax.numpy as jnp
        import numpy as np
        HEADS = 32
        KV_HEADS = 8
        HEAD_DIM = 128
        EPS = 1e-06

        def rms_norm(x, w):
            var = jnp.mean(jnp.square(x.astype(jnp.float32)), axis=-1, keepdims=True)
            return (x.astype(jnp.float32) * jax.lax.rsqrt(var + EPS)).astype(x.dtype) * w
        bsz, q_len, hidden = latents.shape
        kv = jnp.concatenate([context, latents], axis=1)
        kv_len = kv.shape[1]
        groups = HEADS // KV_HEADS
        q = (latents @ Wq).reshape(bsz, q_len, HEADS, HEAD_DIM).transpose(0, 2, 1, 3)
        k = (kv @ Wk).reshape(bsz, kv_len, KV_HEADS, HEAD_DIM).transpose(0, 2, 1, 3)
        v = (kv @ Wv).reshape(bsz, kv_len, KV_HEADS, HEAD_DIM).transpose(0, 2, 1, 3)
        q = rms_norm(q, q_norm_w)
        k = rms_norm(k, k_norm_w)
        qg = q.reshape(bsz, KV_HEADS, groups, q_len, HEAD_DIM)
        scale = 1.0 / np.sqrt(HEAD_DIM)
        scores = jnp.einsum('bhgqd,bhkd->bhgqk', qg, k) * scale
        probs = jax.nn.softmax(scores.astype(jnp.float32), axis=-1).astype(q.dtype)
        out = jnp.einsum('bhgqk,bhkd->bhgqd', probs, v)
        out = out.reshape(bsz, HEADS, q_len, HEAD_DIM).transpose(0, 2, 1, 3)
        out = out.reshape(bsz, q_len, HEADS * HEAD_DIM)
        return out @ Wo

    def _L1_ffn_ref(input, weight, bias):
        import jax, jax.numpy as jnp
        import numpy as np
        B, S, D_IN, D_OUT = (4, 256, 512, 512)
        out = jnp.einsum('bsi,oi->bso', input, weight)
        out = out + bias
        return out
    x = x + jnp.tanh(g_xattn[0]) * _L0_xattn_ref(_layernorm(x, axis=-1), ctx_4096, mask_BxSxS2_bk0, L0_xattn_position_bias, L0_xattn_ln_weight, L0_xattn_w_q, L0_xattn_w_k, L0_xattn_w_v, L0_xattn_w_out)
    x = x + jnp.tanh(g_ffn[0]) * _L0_ffn_ref(_layernorm(x, axis=-1), L0_ffn_qweight, L0_ffn_lut4, L0_ffn_lut8, L0_ffn_bias)
    x = x + jnp.tanh(g_xattn[1]) * _L1_xattn_ref(_layernorm(x, axis=-1), ctx_4096, L1_xattn_Wq, L1_xattn_Wk, L1_xattn_Wv, L1_xattn_Wo, L1_xattn_q_norm_w, L1_xattn_k_norm_w)
    x = x + jnp.tanh(g_ffn[1]) * _L1_ffn_ref(_layernorm(x, axis=-1), L1_ffn_weight, L1_ffn_bias)
    return x

_drawn_inputs = setup_inputs


def setup_inputs(seed=0):
    import zlib

    import numpy as np

    out = dict(_drawn_inputs(seed))
    spreads = {'g_ffn': (-1.0, 0.2),
     'L0_xattn_ln_weight': (1.0, 0.59),
     'L1_xattn_q_norm_w': (1.0, 0.6),
     'L1_xattn_k_norm_w': (1.0, 0.6)}
    factors = {'L0_ffn_bias': 8.0}
    for name, (base, spread) in spreads.items():
        noise = np.random.default_rng([zlib.crc32(name.encode()), seed]).standard_normal(out[name].shape)
        drawn = base * np.exp(spread * noise) if base else spread * noise
        out[name] = jnp.asarray(drawn.astype(out[name].dtype))
    for name, factor in factors.items():
        out[name] = (out[name] * factor).astype(out[name].dtype)
    return out
```

```python
import concourse.bass as bass
from concourse import mybir
from contextlib import ExitStack

fp32 = mybir.dt.float32
fp32r = mybir.dt.float32r
fp16 = mybir.dt.float16
bf16 = mybir.dt.bfloat16
i32 = mybir.dt.int32
u8 = mybir.dt.uint8
ALU = mybir.AluOpType
ACT = mybir.ActivationFunctionType
AX = mybir.AxisListType

P = 128
B = 8
D = 512
C = D // P
H = 32
KV = 8
GQ = H // KV
NG = H // 2
U = 64
FIRST_ORDER = (2, 3, 4, 0, 1)
BODY = 8
TL = U // BODY
LO_BITS, HI_BITS = 4, 8
EST_T = 64.0
EPS_LN, EPS_RMS, EPS_QK = 1e-5, 1e-5, 1e-6
NEG = 1e30
W1 = 5 * 1024


def wait(eng, sem, count):
    if not (isinstance(count, int) and count < 1):
        eng.wait_ge(sem, count)


def build(nc, x, ctx_t, mask, gates, w0, bias0, lnw, qweight, lut4, lut8, ffn0_bias, w1, qk_norm, ffn1_w, ffn1_bias, out):
    stack = ExitStack()
    with stack:
        def sems(names):
            return [stack.enter_context(nc.semaphore(n)) for n in names.split()]

        def keep(name, shape, dt):
            return stack.enter_context(nc.sbuf_tensor(name, shape, dt))

        xr = keep("residual", [P, B, D], fp32)
        xt_hi = keep("xt_hi", [P, C, B * P], fp32r)
        xt_lo = keep("xt_lo", [P, C, B * P], fp32r)
        ct_hi = keep("ct_hi", [P, C, B * P], fp32r)
        ct_lo = keep("ct_lo", [P, C, B * P], fp32r)
        ident = keep("ident", [P, P], fp32)
        fbias = keep("fbias", [P, D], fp32)
        tg = keep("tg", [P, 4], fp32)
        stats = keep("stats", [P, B, 6], fp32)
        mv = keep("mv", [P, B, 2], fp32)
        ve = keep("ve", [P, 2, B], fp32)
        roots = keep("roots", [P, 2, B], fp32)
        rstd, scale0 = roots[:, 0, :], roots[:, 1, :]
        half = keep("half", [P, B], fp32)
        base_s = keep("base_s", [P, B], fp32)
        base_b = keep("base_b", [P, B], fp32)
        qk_w = keep("qk_w", [P, 2], fp32)
        kw = keep("kw", [P, 1], fp32)
        lut = keep("lut", [P, C, 2 ** LO_BITS], fp32)
        codes = keep("codes", [P, 2 ** LO_BITS], fp32)
        shifts = keep("shifts", [P, 32], i32)
        code_now = keep("code_now", [P, 1], fp32)
        norm_sq = keep("norm_sq", [P, B], fp32)
        gate_hi = keep("gate_hi", [P, B], fp32)
        gate_lo = keep("gate_lo", [P, B], fp32)
        any_hi = keep("any_hi", [P, 2], fp32)
        flag = keep("flag", [P, 1], i32)

        phase = ExitStack()

        def tmp(name, shape, dt):
            return phase.enter_context(nc.sbuf_tensor(name, shape, dt))

        wl = tmp("wl", [P, C, D], fp32)
        w0_hi = tmp("w0_hi", [P, 2, 4, 1024], fp32r)
        w0_lo = tmp("w0_lo", [P, 2, 4, 1024], fp32r)
        stage0 = tmp("stage0", [P, 4, 1024], fp32)
        work = tmp("work", [P, 4608], fp32)
        ot0_hi = tmp("ot0_hi", [P, 2, 512], fp32r)
        ot0_lo = tmp("ot0_lo", [P, 2, 512], fp32r)
        negm = tmp("negm", [P, B, P], bf16)
        valid = tmp("valid", [P, B], fp32)
        bias_sb = tmp("bias_sb", [P, 2, 2 * P], fp32)
        eq = tmp("eq", [P, D], fp32)
        idx = tmp("idx", [P, C, D], u8)
        qw = tmp("qw", [P, LO_BITS, C * D // 32], i32)
        nmax = tmp("nmax", [P, 4], fp32)
        ssum = tmp("ssum", [P, 4], fp32)
        rn = tmp("rn", [P, 4], fp32)
        qt, kt = work[:, 0:512], work[:, 512:1024]
        vs = work[:, 1024:2048].rearrange("p (u n) -> p u n", u=2)
        bm = work[:, 2048:3072].rearrange("p (u n) -> p u n", u=2)
        sc, pr, ptr = work[:, 3072:3584], work[:, 3584:4096], work[:, 4096:4608]
        lnw_bc = wl[:, 0, :]
        z0 = [wl[:, 1, :], wl[:, 2, :], wl[:, 3, :]]
        unpacked = wl[:, :, :].bitcast(i32)
        mask_raw = eq[:, :].bitcast(u8)[:, 0:B * P]
        phase.close()

        phase = ExitStack()
        w1_hi = tmp("w1_hi", [P, 2, W1], fp32r)
        w1_lo = tmp("w1_lo", [P, 2, W1], fp32r)
        ot1_hi = tmp("ot1_hi", [P, 512], fp32r)
        ot1_lo = tmp("ot1_lo", [P, 512], fp32r)
        pt_hi = tmp("pt_hi", [P, 2, 512], fp32r)
        pt_lo = tmp("pt_lo", [P, 2, 512], fp32r)
        qt_hi = tmp("qt_hi", [P, 512], fp32r)
        qt_lo = tmp("qt_lo", [P, 512], fp32r)
        kt_hi = tmp("kt_hi", [P, 256], fp32r)
        kt_lo = tmp("kt_lo", [P, 256], fp32r)
        v_hi = tmp("v_hi", [P, 4, 2, P], fp32r)
        v_lo = tmp("v_lo", [P, 4, 2, P], fp32r)
        stage1 = tmp("stage1", [P, 2, 1024], fp32)
        q_sb = tmp("q_sb", [P, 512], fp32)
        q_sq = tmp("q_sq", [P, 512], fp32)
        k_sb = fbias[:, 0:256].rearrange("p (a n) -> p a n", a=2)
        k_sq = fbias[:, 256:512].rearrange("p (a n) -> p a n", a=2)
        p1 = tmp("p1", [P, 4, 256], fp32)
        k_ss = tmp("k_ss", [P, 2], fp32)
        k_ms = tmp("k_ms", [P, 2], fp32)
        k_r = tmp("k_r", [P, 2], fp32)
        q_ss = tmp("q_ss", [P, 4], fp32)
        q_ms = tmp("q_ms", [P, 4], fp32)
        q_r = tmp("q_r", [P, 2, 4], fp32)
        nmax1 = tmp("nmax1", [P, 4], fp32)
        nb1 = tmp("nb1", [P, 4], fp32)
        sum1 = tmp("sum1", [P, 4], fp32)
        rn1 = tmp("rn1", [P, 4], fp32)
        fbias16 = stage1[:, :, :].bitcast(fp16)[:, 1, 0:D]
        phase.close()

        phase = ExitStack()
        tmp("below_second_low_weights", [P, C * D + 8 * 1024 + 4 * 1024], fp32)
        ctx_stage = tmp("ctx_stage", [P, B // 2, C * 2 * P], fp32)
        ctx_raw = [ctx_stage[:, p, :].rearrange("p (c n) -> p c n", c=C) for p in range(B // 2)]
        phase.close()

        phase = ExitStack()
        tmp("high_weights_of_layer_1", [P, 2 * W1], fp32)
        plain1 = tmp("plain1", [P, W1], fp32)
        phase.close()

        phase = ExitStack()
        tmp("weights_of_layer_1", [P, 2 * 2 * W1], fp32)
        z_mid = tmp("z_mid", [P, 4, D], fp32)
        wl8 = tmp("wl8", [P, C, D], fp32)
        eq8 = tmp("eq8", [P, D], fp32)
        idx8 = tmp("idx8", [P, C, D], u8)
        qw8 = tmp("qw8", [P, HI_BITS, C * D // 32], i32)
        lut8_sb = tmp("lut8_sb", [P, C, 2 ** HI_BITS], fp32)
        phase.close()
        by_chunk = lambda ap: ap.rearrange("p (c n) -> p c n", c=C)
        fw_hi, fw_lo = by_chunk(w1_hi[:, 1, 0:2048]), by_chunk(w1_lo[:, 1, 0:2048])
        fw8_hi, fw8_lo = by_chunk(w1_hi[:, 1, 2048:4096]), by_chunk(w1_lo[:, 1, 2048:4096])
        fw1 = by_chunk(w1_hi[:, 0, 0:2048])
        fbias1 = plain1[:, 4096:4096 + D]

        def z_rows(phase_no, b):
            if phase_no == 0:
                return z0[b % 3]
            if phase_no < 3:
                return z_mid[:, b % 4, :]
            return plain1[:, D * b:D * (b + 1)]

        WLT_BANK = (0, 1, 2, 0)
        XT_BANK = [(3, 4, 6, 7, 4, 5, 6, 7), (0, 1) * 4, (4, 5, 6, 7) * 2, (0, 1) * 4]

        bank = [stack.enter_context(nc.psum_tensor(f"bank{n}", [P, 512], fp32)) for n in range(8)]
        QB, KB, VB, SB, TB, OB, YA, YB = bank
        KVB, Q1B, S0B, S1B, T0B, T1B, O1B, Y1B = bank

        (x_in0, x_in1, x_in2, x_in3, x_in4, x_in5, x_in6, x_in7) = x_in = sems(" ".join(f"x_in{b}" for b in range(B)))
        gate_in, lnw_in, mask_in, quant_in, fbias_in, const_done = sems(
            "gate_in lnw_in mask_in quant_in fbias_in const_done")
        chain, ident_done, half_done = sems("chain ident_done half_done")
        ctx_hi_done, ctx_lo_done, tanh_done, negm_done, valid_done = sems(
            "ctx_hi_done ctx_lo_done tanh_done negm_done valid_done")
        (ve_done, rstd_done, z_done, xt_ps, xt_hi_done, xt_lo_done) = sems(
            "ve_done rstd_done z_done xt_ps xt_hi_done xt_lo_done")
        z_scaled, z0_done = sems("z_scaled z0_done")
        base_ready, base_done, biased = sems("base_ready base_done biased")
        first_in, first_hi, first_lo = sems("first_in first_hi first_lo")
        (q_ps, k_ps, v_ps, s_ps, pt_ps, o_ps, y_ps) = sems("q_ps k_ps v_ps s_ps pt_ps o_ps y_ps")
        (qt_done, kt_done, v_done, exp_done, ot_hi_done) = sems("qt_done kt_done v_done exp_done ot_hi_done")
        (added, max_done, recip_done, rn_done, pt_done, ot_lo_done, acc_done) = sems(
            "added max_done recip_done rn_done pt_done ot_lo_done acc_done")
        (bm_done, norm_done) = sems("bm_done norm_done")
        ctx_in = sems(" ".join(f"ctx_in{p}" for p in range(B // 2)))
        w_in, w_hi_done, w_lo_done = (sems(" ".join(f"{n}{w}" for w in "qkvo")) for n in ("w_in_", "w_hi_", "w_lo_"))
        bias_in = sems("bias_in_even bias_in_odd")
        eq_done, wl_done = sems("eq_done wl_done")
        wlt_ps, fw_hi_done, fw_lo_done, fw_in = sems("wlt_ps fw_hi_done fw_lo_done fw_in")
        fy_ps, facc_done, out_done = sems("fy_ps facc_done out_done")
        w1_in, w1_hi_done, w1_lo_done = (sems(" ".join(f"{n}{w}" for w in range(5))) for n in ("w1_in_", "w1_hi_", "w1_lo_"))
        kv1, q1, tk1, tq1, s1, d1, o1, y1 = sems("kv1 q1 tk1 tq1 s1 d1 o1 y1")
        (ksq1, qc1, qsq1, qh1, kh1, e1, ph1, oh1) = sems("ksq1 qc1 qsq1 qh1 kh1 e1 ph1 oh1")
        (vl1, kms1, ks1, qss1, qms1, ql1, kl1, nm1, nb1s, rn1s, pl1, ol1, acc1) = sems(
            "vl1 kms1 ks1 qss1 qms1 ql1 kl1 nm1 nb1s rn1s pl1 ol1 acc1")
        kr1, qr1, pn1a, pn1b, qrs1 = sems("kr1 qr1 pn1a pn1b qrs1")
        (qk_in,) = sems("qk_in")
        any_done, all_done, flag_done = sems("any_done all_done flag_done")
        hi_in, hi_eq, hi_add, hi_chain, hi_wt, hi_fw_hi, hi_fw_lo, hi_y, hi_acc = sems(
            "hi_in hi_eq hi_add hi_chain hi_wt hi_fw_hi hi_fw_lo hi_y hi_acc")

        block = stack.enter_context(nc.Block())
        tok = lambda b: slice(b * P, (b + 1) * P)
        by4 = lambda ap: ap.rearrange("p (a n) -> p a n", a=4)
        by2 = lambda ap: ap.rearrange("p (a n) -> p a n", a=2)

        def some_high(eng):
            eng.wait_ge(flag_done, 1)
            return eng.value_load(flag[0:1, 0:1], min_val=0, max_val=1)

        @block.sync
        def _(sp):
            sp.dma_start(tg[:, :], gates.to_broadcast([P, 4])).then_inc(gate_in, 16)
            def load_context(p):
                sp.dma_start(ctx_raw[p], ctx_t[:, :, 2 * p * P:2 * (p + 1) * P]).then_inc(ctx_in[p], 16)

            def load_first(w):
                sp.dma_start(stage0[:, w, :], w0[0, w, :, :]).then_inc(w_in[w], 16)

            def load_rows(b):
                sp.dma_start(xr[:, b, :], x[b, :, :]).then_inc(x_in[b], 16)

            load_first(1)
            load_context(0)
            load_rows(0)
            load_rows(1)
            sp.dma_start(lnw_bc, lnw.to_broadcast([P, D])).then_inc(lnw_in, 16)
            load_first(2)
            load_first(0)
            load_rows(2)
            load_rows(3)
            load_context(1)
            load_rows(4)
            load_rows(5)
            sp.dma_start(eq[:, 0:B * P // 4].bitcast(i32), mask).then_inc(mask_in, 16)
            for n in range(2):
                sp.dma_start(bias_sb[:, n, :], bias0[n, :, :]).then_inc(bias_in[n], 16)
            load_rows(6)
            load_rows(7)
            load_context(2)
            load_first(3)
            load_context(3)
            sp.dma_start(qw[:, :, :], qweight[:, 0:LO_BITS, :]).then_inc(quant_in, 16)
            sp.dma_start(lut[:, :, :], lut4).then_inc(quant_in, 16)
            sp.dma_start(fbias[:, :], ffn0_bias.to_broadcast([P, D])).then_inc(fbias_in, 16)
            sp.dma_start(qk_w[:, :], qk_norm).then_inc(qk_in, 16)

            def load_group(n):
                for w in range(4):
                    sp.wait_ge(w_lo_done[w], n + 1)
                    sp.dma_start(stage0[:, w, :], w0[n + 1, w, :, :]).then_inc(w_in[w], 16)

            def load_bias(n, parity):
                sp.wait_ge(bm_done, 4 * (n + 1))
                sp.dma_start(bias_sb[:, parity, :], bias0[n + 2, :, :]).then_inc(bias_in[parity], 16)

            with sp.Fori(0, NG // 2 - 1) as t:
                for parity in range(2):
                    load_group(2 * t + parity)
                    load_bias(2 * t + parity, parity)
            load_group(NG - 2)

            for piece, used, count in ((0, q_ps, U - 4), (1, k_ps, U - 4), (2, v_ps, U - 4), (3, y_ps, U - 4), (4, q_ps, U)):
                sp.wait_ge(used, count)
                sp.dma_start(plain1[:, 1024 * piece:1024 * (piece + 1)], w1[0, piece, :, :]).then_inc(first_in, 16)

            def load1(n, piece):
                sp.dma_start(stage1[:, piece % 2, :], w1[n, piece, :, :]).then_inc(w1_in[piece], 16)

            sp.wait_ge(acc_done, U)
            load1(1, 0)
            load1(1, 1)
            with sp.If(some_high(sp)):
                sp.dma_start(qw8[:, :, :], qweight).then_inc(hi_in, 16)
                sp.dma_start(lut8_sb[:, :, :], lut8).then_inc(hi_in, 16)
            for piece in range(2, 5):
                sp.wait_ge(w1_lo_done[piece - 2], 1)
                load1(1, piece)
            with sp.Fori(2, KV) as n:
                for piece, before, count in ((0, 4, n - 1), (1, 3, n - 1), (2, 0, n), (3, 1, n), (4, 2, n)):
                    sp.wait_ge(w1_lo_done[before], count)
                    load1(n, piece)

            sp.wait_ge(w1_lo_done[4], KV - 1)
            sp.wait_ge(w1_lo_done[3], KV - 1)
            sp.dma_start(stage1[:, :, :].bitcast(fp16)[:, 0, :], ffn1_w).then_inc(fw_in, 16)
            sp.dma_start(fbias16, ffn1_bias.to_broadcast([P, D])).then_inc(fbias_in, 16)
            for b in range(B):
                sp.wait_ge(facc_done, B + b + 1)
                sp.dma_start(out[b, :, :], xr[:, b, :]).then_inc(out_done, 16)
            sp.wait_ge(out_done, 16 * B)

        @block.gpsimd
        def _(pool):
            pool.memset(ident[:, :], 0.0).then_inc(ident_done, 1)
            pool.memset(half[:, :], -0.5).then_inc(half_done, 1)
            pool.wait_ge(ident_done, 1)
            pool.affine_select(out=ident[:, :], in_=ident[:, :], compare_op=ALU.not_equal, fill=1.0, base=0,
                               pattern=[[-1, P]], channel_multiplier=1).then_inc(ident_done, 1)
            pool.iota(shifts[:, :], pattern=[[1, 32]], base=0, channel_multiplier=0).then_inc(const_done, 1)

            def rsqrt(dst, src, exponent, ready, count, done):
                pool.wait_ge(ready, count)
                pool.tensor_tensor(dst, src, exponent, ALU.pow).then_inc(done, 1)

            def row_roots(phase_no, p):
                both, pair = (2 if phase_no == 0 else 1), slice(2 * p, 2 * p + 2)
                rsqrt(roots[:, 0:both, pair], ve[:, 0:both, pair], half[:, 0:2 * both].rearrange("p (a n) -> p a n", a=both),
                      ve_done, 4 * phase_no + p + 1, rstd_done)

            def add_bias(phase_no, b, row):
                pool.wait_ge(z_done, B * (phase_no - 1) + b + 1)
                pool.tensor_tensor(xr[:, b, :], xr[:, b, :], row, ALU.add).then_inc(biased, 1)

            def weighted(b):
                pool.wait_ge(z_scaled, b + 1)
                pool.tensor_tensor(z_rows(0, b), z_rows(0, b), lnw_bc, ALU.mult).then_inc(z0_done, 1)

            pool.wait_ge(half_done, 1)
            pool.wait_ge(lnw_in, 16)
            row_roots(0, 0)
            weighted(0)
            weighted(1)
            row_roots(0, 1)
            weighted(2)
            weighted(3)
            row_roots(0, 2)
            weighted(4)
            weighted(5)
            pool.wait_ge(negm_done, 1)

            def slot(t, j, tail=False):
                i, n, p, parity = BODY * t + j, 2 * t + j // 4, j % 4, (j // 4) % 2
                first = isinstance(t, int) and t == 0
                last = isinstance(t, int) and t == TL - 1
                if not tail:
                    if p == 0:
                        pool.wait_ge(bias_in[parity], 16 * (t + 1))
                    wait(pool, added, i - 1)
                    pool.tensor_tensor(
                        by4(bm[:, i % 2 if isinstance(t, int) else j % 2, :]).rearrange("p (h b) k -> p h b k", h=2),
                        by2(bias_sb[:, parity, :]).unsqueeze(2).to_broadcast([P, 2, 2, P]),
                        negm[:, 2 * p:2 * p + 2, :].unsqueeze(1).to_broadcast([P, 2, 2, P]),
                        ALU.add).then_inc(bm_done, 1)
                if not (first and j == 0):
                    pool.wait_ge(rn_done, i)
                    pool.tensor_tensor(by4(pr), by4(pr), rn[:, :].unsqueeze(2).to_broadcast([P, 4, P]),
                                       ALU.mult).then_inc(norm_done, 1)
                if first and j == 0:
                    row_roots(0, 3)
                    weighted(6)
                    weighted(7)
                if first and 1 <= j <= B // 2:
                    pool.wait_ge(base_ready, 2)
                    for b in (2 * j - 2, 2 * j - 1):
                        pool.tensor_scalar(xr[:, b, :], xr[:, b, :], base_s[:, b:b + 1], base_b[:, b:b + 1],
                                           ALU.mult, ALU.add).then_inc(base_done, 1)

            for j in range(BODY):
                slot(0, j)
            with pool.Fori(1, TL - 1) as t:
                for j in range(BODY):
                    slot(t, j)
            for j in range(BODY):
                slot(TL - 1, j)
            slot(TL - 1, BODY, tail=True)

            def first_low(k):
                piece = FIRST_ORDER[k]
                cols = slice(1024 * piece, 1024 * (piece + 1))
                pool.wait_ge(first_hi, k + 1)
                pool.tensor_tensor(w1_lo[:, 0, cols], plain1[:, cols], w1_hi[:, 0, cols].bitcast(fp32),
                                   ALU.subtract).then_inc(first_lo, 1)

            row_roots(1, 0)
            first_low(0)
            first_low(1)
            row_roots(1, 1)
            add_bias(1, 0, fbias[:, :])
            add_bias(1, 1, fbias[:, :])
            row_roots(1, 2)
            add_bias(1, 2, fbias[:, :])
            add_bias(1, 3, fbias[:, :])
            row_roots(1, 3)
            add_bias(1, 4, fbias[:, :])
            add_bias(1, 5, fbias[:, :])
            pool.wait_ge(any_done, 1)
            pool.partition_all_reduce(any_hi[:, 1:2], any_hi[:, 0:1], P, bass.bass_isa.ReduceOp.max).then_inc(all_done, 1)
            first_low(2)
            add_bias(1, 6, fbias[:, :])
            add_bias(1, 7, fbias[:, :])
            first_low(3)
            row_roots(2, 0)
            first_low(4)
            row_roots(2, 1)
            row_roots(2, 2)
            row_roots(2, 3)

            def k_root(count):
                rsqrt(k_r[:, :], k_ms[:, :], half[:, 0:2], kms1, count, kr1)

            def q_root(count, parity):
                rsqrt(q_r[:, parity, :], q_ms[:, :], half[:, 0:4], qms1, count, qr1)

            k_root(1)
            q_root(1, 0)

            def slot1(t, j, tail=False):
                i = BODY * t + j
                first = isinstance(t, int) and t == 0
                last = isinstance(t, int) and t == TL - 1
                if not (first and j == 0):
                    pool.wait_ge(rn1s, i)
                    for half_p, done in ((0, pn1a), (2, pn1b)):
                        pool.tensor_tensor(p1[:, half_p:half_p + 2, :], p1[:, half_p:half_p + 2, :],
                                           rn1[:, half_p:half_p + 2].unsqueeze(2).to_broadcast([P, 2, 256]),
                                           ALU.mult).then_inc(done, 1)
                if not tail and not (last and j == BODY - 1):
                    k_root(i + 2)
                    q_root(i + 2, (j + 1) % 2)
                if last and not tail:
                    if j in (5, 7):
                        for b in (j - 5, j - 4):
                            add_bias(3, b, fbias1)
                    if j in (3, 5, 7):
                        row_roots(3, (j - 3) // 2)

            for j in range(BODY):
                slot1(0, j)
            with pool.Fori(1, TL - 1) as t:
                for j in range(BODY):
                    slot1(t, j)
            for j in range(BODY):
                slot1(TL - 1, j)
            slot1(TL - 1, BODY, tail=True)
            add_bias(3, 4, fbias1)
            add_bias(3, 5, fbias1)
            row_roots(3, 3)
            add_bias(3, 6, fbias1)
            add_bias(3, 7, fbias1)

        @block.scalar
        def _(act):
            act.wait_ge(gate_in, 16)
            nc.scalar.activation(tg[:, :], tg[:, :], ACT.Tanh).then_inc(tanh_done, 1)

            def transposed_hi(phase_no, b):
                act.wait_ge(xt_ps, B * phase_no + b + 1)
                nc.scalar.activation(xt_hi[:, :, tok(b)], by4(bank[XT_BANK[phase_no][b]][:, :]),
                                     ACT.Copy).then_inc(xt_hi_done, 1)

            def first_weight(w):
                act.wait_ge(w_in[w], 16)
                nc.scalar.activation(w0_hi[:, 0, w, :], stage0[:, w, :], ACT.Copy).then_inc(w_hi_done[w], 1)

            def context_hi(p):
                act.wait_ge(ctx_in[p], 16)
                nc.scalar.activation(ct_hi[:, :, 2 * p * P:2 * (p + 1) * P], ctx_raw[p], ACT.Copy).then_inc(ctx_hi_done, 1)

            first_weight(1)
            context_hi(0)
            first_weight(2)
            first_weight(0)
            transposed_hi(0, 0)
            transposed_hi(0, 1)
            context_hi(1)
            transposed_hi(0, 2)
            transposed_hi(0, 3)

            def exponentials(count):
                act.wait_ge(max_done, count)
                wait(act, pt_ps, count - 1)
                for a in range(4):
                    last_op = nc.scalar.activation(by4(pr)[:, a, :], by4(sc)[:, a, :], ACT.Exp,
                                                   bias=nmax[:, a:a + 1], accum_out=ssum[:, a:a + 1])
                last_op.then_inc(exp_done, 1)

            def output_hi(count, j):
                act.wait_ge(o_ps, count)
                wait(act, y_ps, count - 2)
                nc.scalar.activation(ot0_hi[:, j % 2, :], OB[:, :], ACT.Copy).then_inc(ot_hi_done, 1)

            def slot(t, j):
                i, n, p, parity = BODY * t + j, 2 * t + j // 4, j % 4, (j // 4) % 2
                first = isinstance(t, int) and t == 0
                last = isinstance(t, int) and t == TL - 1
                if not (first and j == 0):
                    exponentials(i)
                def next_weight():
                    act.wait_ge(w_in[p], 16 * (n + 2))
                    wait(act, (q_ps, k_ps, v_ps, y_ps)[p], 4 * n)
                    nc.scalar.activation(w0_hi[:, 1 - parity, p, :], stage0[:, p, :], ACT.Copy).then_inc(w_hi_done[p], 1)

                if not (last and j >= 4) and not (first and j == 0):
                    next_weight()
                act.wait_ge(q_ps, i + 1)
                wait(act, s_ps, i)
                nc.scalar.activation(qt, QB[:, :], ACT.Copy).then_inc(qt_done, 1)
                act.wait_ge(k_ps, i + 1)
                nc.scalar.activation(kt, KB[:, :], ACT.Copy).then_inc(kt_done, 1)
                act.wait_ge(v_ps, i + 1)
                wait(act, o_ps, i - 1)
                nc.scalar.activation(vs[:, j % 2, :], VB[:, :], ACT.Copy).then_inc(v_done, 1)
                if not (first and j == 0):
                    output_hi(i, j - 1)
                if first and j < 2:
                    transposed_hi(0, 2 * j + 4)
                    transposed_hi(0, 2 * j + 5)
                    context_hi(j + 2)
                    if j == 0:
                        first_weight(3)
                        next_weight()

            for j in range(BODY):
                slot(0, j)
            with act.Fori(1, TL - 1) as t:
                for j in range(BODY):
                    slot(t, j)
            for j in range(BODY):
                slot(TL - 1, j)

            def weight_hi(c):
                act.wait_ge(wlt_ps, c + 1)
                nc.scalar.activation(fw_hi[:, c, :], bank[WLT_BANK[c]][:, :], ACT.Copy).then_inc(fw_hi_done, 1)

            def first_rounded(k):
                piece = FIRST_ORDER[k]
                cols = slice(1024 * piece, 1024 * (piece + 1))
                act.wait_ge(first_in, 16 * 5)
                if k == 3:
                    act.wait_ge(wlt_ps, C)
                nc.scalar.activation(w1_hi[:, 0, cols], plain1[:, cols], ACT.Copy).then_inc(first_hi, 1)

            weight_hi(0)
            weight_hi(1)
            exponentials(U)
            weight_hi(2)
            weight_hi(3)
            first_rounded(0)
            first_rounded(1)
            output_hi(U, BODY - 1)
            first_rounded(2)
            transposed_hi(1, 0)
            transposed_hi(1, 1)
            first_rounded(3)
            first_rounded(4)
            for b in range(2, B):
                transposed_hi(1, b)
            with act.If(some_high(act)):
                for c in range(C):
                    act.wait_ge(hi_wt, c + 1)
                    nc.scalar.activation(fw8_hi[:, c, :], bank[4 + c][:, :], ACT.Copy).then_inc(hi_fw_hi, 1)
            transposed_hi(2, 0)
            transposed_hi(2, 1)

            def kv_out(count, place):
                act.wait_ge(kv1, count)
                kv = by2(KVB[:, :])
                nc.scalar.activation(v_hi[:, place, :, :], kv[:, :, P:2 * P], ACT.Copy)
                for tile in range(2):
                    last_op = nc.scalar.activation(k_sq[:, tile, :], kv[:, tile, 0:P], ACT.Square,
                                                   accum_out=k_ss[:, tile:tile + 1])
                last_op.then_inc(ksq1, 1)

            def q_out(count):
                act.wait_ge(q1, count)
                nc.scalar.activation(q_sb[:, :], Q1B[:, :], ACT.Copy).then_inc(qc1, 1)
                nc.scalar.activation(q_sq[:, :], Q1B[:, :], ACT.Square).then_inc(qsq1, 1)

            act.wait_ge(biased, B)
            kv_out(1, 0)
            q_out(1)

            def exponentials1(count, parity):
                act.wait_ge(nb1s, count)
                wait(act, d1, count - 1)
                for a in range(4):
                    last_op = nc.scalar.activation(p1[:, a, :], by2((S0B, S1B)[a // 2][:, :])[:, a % 2, :], ACT.Exp,
                                                   bias=nb1[:, a:a + 1], scale=q_r[:, parity, a:a + 1],
                                                   accum_out=sum1[:, a:a + 1])
                last_op.then_inc(e1, 1)

            def probabilities_hi(count):
                act.wait_ge(d1, count)
                wait(act, o1, count - 1)
                for kc in range(2):
                    last_op = nc.scalar.activation(pt_hi[:, kc, :], (T0B, T1B)[kc][:, :], ACT.Copy)
                last_op.then_inc(ph1, 1)

            def output1_hi(count):
                act.wait_ge(o1, count)
                wait(act, y1, count - 1)
                nc.scalar.activation(ot1_hi[:, :], O1B[:, :], ACT.Copy).then_inc(oh1, 1)

            def slot1(t, j):
                i = BODY * t + j
                first = isinstance(t, int) and t == 0
                last = isinstance(t, int) and t == TL - 1
                act.wait_ge(tq1, i + 1)
                nc.scalar.activation(qt_hi[:, :], Q1B[:, :], ACT.Copy).then_inc(qh1, 1)
                act.wait_ge(tk1, i + 1)
                nc.scalar.activation(kt_hi[:, :], KVB[:, 0:256], ACT.Copy, scale=kw[:, 0:1]).then_inc(kh1, 1)
                if first and j == 0:
                    transposed_hi(2, 2)
                    transposed_hi(2, 3)
                if not (first and j == 0):
                    exponentials1(i, (j - 1) % 2)
                if not (last and j == BODY - 1):
                    wait(act, o1, i - 2)
                    kv_out(i + 2, (j + 1) % 4)
                if first and j == 0:
                    transposed_hi(2, 4)
                    transposed_hi(2, 5)
                if not (first and j == 0):
                    probabilities_hi(i)
                if not (last and j == BODY - 1):
                    q_out(i + 2)
                if first and j == 0:
                    transposed_hi(2, 6)
                    transposed_hi(2, 7)
                if not (first and j == 0):
                    output1_hi(i)
                if last and j >= 4:
                    act.wait_ge(fw_in, 16)
                    act.wait_ge(y1, U - BODY)
                    nc.scalar.activation(fw1[:, j - 4, :], by4(stage1[:, :, :].bitcast(fp16)[:, 0, :])[:, j - 4, :],
                                         ACT.Copy).then_inc(fw_hi_done, 1)

            for j in range(BODY):
                slot1(0, j)
            with act.Fori(1, TL - 1) as t:
                for j in range(BODY):
                    slot1(t, j)
            for j in range(BODY):
                slot1(TL - 1, j)
            exponentials1(U, (BODY - 1) % 2)
            transposed_hi(3, 0)
            transposed_hi(3, 1)
            probabilities_hi(U)
            transposed_hi(3, 2)
            transposed_hi(3, 3)
            output1_hi(U)
            for b in range(4, B):
                transposed_hi(3, b)

        @block.vector
        def _(dve):
            steps = [0]

            def link(op):
                steps[0] += 1
                op.then_inc(chain, 1)
                dve.wait_ge(chain, steps[0])

            def row_stats(phase_no, p):
                pair = slice(2 * p, 2 * p + 2)
                for b in (2 * p, 2 * p + 1):
                    if phase_no == 0:
                        dve.wait_ge(x_in[b], 16)
                    last_op = nc.vector.bn_stats(stats[:, b, :], xr[:, b, :])
                link(last_op)
                for b in (2 * p, 2 * p + 1):
                    last_op = nc.vector.bn_aggr(mv[:, b, :], stats[:, b, :])
                link(last_op)
                op = nc.vector.tensor_scalar(ve[:, 0, pair], mv[:, pair, 1], EPS_LN, None, ALU.add)
                if phase_no == 0:
                    link(op)
                    op = nc.vector.scalar_tensor_tensor(out=ve[:, 1, pair], in0=ve[:, 0, pair], scalar=EPS_RMS,
                                                        in1=mv[:, pair, 1], op0=ALU.mult, op1=ALU.add)
                op.then_inc(ve_done, 1)

            def transposed_lo(phase_no, b):
                dve.wait_ge(xt_hi_done, B * phase_no + b + 1)
                nc.vector.tensor_tensor(xt_lo[:, :, tok(b)], by4(bank[XT_BANK[phase_no][b]][:, :]),
                                        xt_hi[:, :, tok(b)].bitcast(fp32), ALU.subtract).then_inc(xt_lo_done, 1)

            def normed_rows(phase_no, b):
                dve.wait_ge(rstd_done, 4 * phase_no + b // 2 + 1)
                wait(dve, xt_ps, B * phase_no + b + 1 - {0: 3, 3: B}.get(phase_no, 4))
                scale, done = (scale0, z_scaled) if phase_no == 0 else (rstd, z_done)
                nc.vector.tensor_scalar(z_rows(phase_no, b), xr[:, b, :], mv[:, b, 0:1], scale[:, b:b + 1],
                                        ALU.subtract, ALU.mult).then_inc(done, 1)

            def first_weight_lo(w):
                dve.wait_ge(w_hi_done[w], 1)
                nc.vector.tensor_tensor(w0_lo[:, 0, w, :], stage0[:, w, :], w0_hi[:, 0, w, :].bitcast(fp32),
                                        ALU.subtract).then_inc(w_lo_done[w], 1)

            def context_lo(p):
                pair = slice(2 * p * P, 2 * (p + 1) * P)
                dve.wait_ge(ctx_hi_done, p + 1)
                nc.vector.tensor_tensor(ct_lo[:, :, pair], ctx_raw[p], ct_hi[:, :, pair].bitcast(fp32),
                                        ALU.subtract).then_inc(ctx_lo_done, 1)

            first_weight_lo(1)
            context_lo(0)
            row_stats(0, 0)
            first_weight_lo(2)
            normed_rows(0, 0)
            normed_rows(0, 1)
            first_weight_lo(0)
            row_stats(0, 1)
            transposed_lo(0, 0)
            transposed_lo(0, 1)
            normed_rows(0, 2)
            normed_rows(0, 3)
            row_stats(0, 2)
            context_lo(1)
            dve.wait_ge(mask_in, 16)
            by_batch = mask_raw.rearrange("p (b k) -> p b k", b=B)
            nc.vector.tensor_scalar(negm[:, :, :], by_batch, NEG, -NEG, ALU.mult, ALU.add).then_inc(negm_done, 1)
            normed_rows(0, 4)
            transposed_lo(0, 2)
            normed_rows(0, 5)
            transposed_lo(0, 3)

            def residual_factors():
                dve.wait_ge(tanh_done, 1)
                dve.wait_ge(rstd_done, 4)
                link(nc.vector.tensor_tensor(base_b[:, :], mv[:, :, 0], rstd[:, :], ALU.mult))
                nc.vector.tensor_scalar(base_s[:, :], rstd[:, :], tg[:, 0:1], 1.0, ALU.mult, ALU.add).then_inc(base_ready, 1)
                link(nc.vector.tensor_scalar(base_b[:, :], base_b[:, :], -1.0, None, ALU.mult))
                nc.vector.tensor_scalar(base_b[:, :], base_b[:, :], tg[:, 0:1], None, ALU.mult).then_inc(base_ready, 1)

            def dequantising_constants():
                dve.wait_ge(fbias_in, 16)
                link(nc.vector.tensor_scalar(fbias[:, :], fbias[:, :], tg[:, 2:3], None, ALU.mult))
                dve.wait_ge(quant_in, 32)
                dve.wait_ge(const_done, 1)
                dve.wait_ge(qk_in, 16)
                nc.vector.tensor_copy(codes[:, :], shifts[:, 0:2 ** LO_BITS])
                nc.vector.tensor_tensor(kw[:, :], qk_w[:, 0:1], qk_w[:, 1:2], ALU.mult)
                link(nc.vector.memset(idx[:, :, :], 0))

            def unpack(plane, steps, packed=qw, scratch=unpacked, index=idx, link=link):
                words = packed[:, plane, :].unsqueeze(2).to_broadcast([P, C * D // 32, 32])
                bits = scratch.rearrange("p c (w s) -> p (c w) s", s=32)
                flat = scratch.rearrange("p c n -> p (c n)")
                codes8 = index[:, :, :].rearrange("p c n -> p (c n)")
                if "shift" in steps:
                    link(nc.vector.tensor_tensor(bits, words, shifts[:, :].unsqueeze(1).to_broadcast([P, C * D // 32, 32]),
                                                 ALU.logical_shift_right))
                if "mask" in steps:
                    link(nc.vector.tensor_scalar(flat, flat, 1, None, ALU.bitwise_and))
                if "add" in steps:
                    link(nc.vector.scalar_tensor_tensor(out=codes8, in0=flat, scalar=float(1 << plane), in1=codes8,
                                                        op0=ALU.mult, op1=ALU.add))

            UNPACK = {(2, "end"): (0, "shift"), (3, "middle"): (0, "mask"), (3, "end"): (0, "add"),
                      (4, "middle"): (1, "shift"), (4, "end"): (1, "mask"), (5, "middle"): (1, "add"),
                      (5, "end"): (2, "shift"), (6, "middle"): (2, "mask add"), (6, "end"): (3, "shift"),
                      (7, "middle"): (3, "mask"), (7, "end"): (3, "add")}

            def dequantise(code, c, count):
                wait(dve, wl_done, count - 1)
                nc.vector.tensor_scalar(eq[:, :], idx[:, c, :], codes[:, bass.ds(code, 1)],
                                        lut[:, c, bass.ds(code, 1)], ALU.is_equal, ALU.mult).then_inc(eq_done, 1)
                dve.wait_ge(eq_done, count)
                nc.vector.tensor_tensor(wl[:, c, :], wl[:, c, :], eq[:, :], ALU.add).then_inc(wl_done, 1)

            def maxima(count, parity):
                dve.wait_ge(s_ps, count)
                dve.wait_ge(bm_done, count)
                wait(dve, exp_done, count - 1)
                nc.vector.tensor_tensor(sc, SB[:, :], bm[:, parity, :], ALU.add).then_inc(added, 1)
                dve.wait_ge(added, count)
                nc.vector.tensor_reduce(nmax[:, :], by4(sc), axis=AX.X, op=ALU.max, negate=True).then_inc(max_done, 1)

            def accumulate(count, pair):
                dve.wait_ge(y_ps, count)
                nc.vector.scalar_tensor_tensor(out=xr[:, pair, :], in0=YA[:, :], scalar=tg[:, 0:1],
                                               in1=xr[:, pair, :], op0=ALU.mult, op1=ALU.add)
                nc.vector.scalar_tensor_tensor(out=xr[:, pair + 1, :], in0=YB[:, :], scalar=tg[:, 0:1],
                                               in1=xr[:, pair + 1, :], op0=ALU.mult, op1=ALU.add).then_inc(acc_done, 1)

            def inverse_sums(count, pair):
                dve.wait_ge(exp_done, count)
                nc.vector.reciprocal(rn[:, :], ssum[:, :]).then_inc(recip_done, 1)
                dve.wait_ge(recip_done, count)
                nc.vector.tensor_tensor(by2(rn[:, :]), by2(rn[:, :]),
                                        valid[:, pair:pair + 2].unsqueeze(1).to_broadcast([P, 2, 2]),
                                        ALU.mult).then_inc(rn_done, 1)

            def probabilities_out(count):
                dve.wait_ge(pt_ps, count)
                wait(dve, o_ps, count - 1)
                nc.vector.tensor_copy(ptr, TB[:, :]).then_inc(pt_done, 1)

            def output_lo(count, parity):
                dve.wait_ge(ot_hi_done, count)
                nc.vector.tensor_tensor(ot0_lo[:, parity, :], OB[:, :], ot0_hi[:, parity, :].bitcast(fp32),
                                        ALU.subtract).then_inc(ot_lo_done, 1)

            def slot(t, j):
                i, n, p, parity = BODY * t + j, 2 * t + j // 4, j % 4, (j // 4) % 2
                first = isinstance(t, int) and t == 0
                last = isinstance(t, int) and t == TL - 1
                lag1 = not (first and j < 1)

                def next_weight_lo(w):
                    dve.wait_ge(w_hi_done[w], n + 2)
                    if first and j < B // 2:
                        dve.wait_ge(ctx_lo_done, w + 1)
                    nc.vector.tensor_tensor(w0_lo[:, 1 - parity, w, :], stage0[:, w, :],
                                            w0_hi[:, 1 - parity, w, :].bitcast(fp32),
                                            ALU.subtract).then_inc(w_lo_done[w], 1)

                if lag1:
                    maxima(i, (j - 1) % 2)
                if not (first and j < 3):
                    if first and j < 3 + B // 2:
                        dve.wait_ge(base_done, 2 * (j - 3) + 2)
                    accumulate(i - 2, 2 * ((j - 3) % 4))
                if first and j == 1:
                    transposed_lo(0, 4)
                    transposed_lo(0, 5)
                    nc.vector.tensor_reduce(valid[:, :], by_batch, axis=AX.X, op=ALU.max).then_inc(valid_done, 1)
                    dve.wait_ge(valid_done, 1)
                if lag1:
                    inverse_sums(i, 2 * ((j - 1) % 4))
                if first and j == 0:
                    row_stats(0, 3)
                    normed_rows(0, 6)
                    normed_rows(0, 7)
                if not (last and j >= 4) and not (first and j == 0):
                    next_weight_lo(p)
                if first and j == 1:
                    residual_factors()
                    dequantising_constants()
                if first and j == 2:
                    first_weight_lo(3)
                    context_lo(3)
                if first and (j, "middle") in UNPACK:
                    unpack(*UNPACK[j, "middle"])
                if lag1:
                    probabilities_out(i)
                    output_lo(i, (j - 1) % 2)
                if first:
                    if j == 1:
                        context_lo(2)
                        transposed_lo(0, 6)
                        transposed_lo(0, 7)
                        next_weight_lo(0)
                    elif j >= 2:
                        unpack(*UNPACK[j, "end"])
                    if j == BODY - 1:
                        link(nc.vector.memset(wl[:, :, :], 0.0))
                elif not last:
                    dequantise(2 * (t - 1) + j // 4, j % 4, BODY * (t - 1) + j + 1)
                else:
                    for k in range(2):
                        dequantise(2 * (TL - 2 + k) + j // 4, j % 4, BODY * (TL - 2) + 2 * j + k + 1)

            for j in range(BODY):
                slot(0, j)
            with dve.Fori(1, TL - 1) as t:
                for j in range(BODY):
                    slot(t, j)
            for j in range(BODY):
                slot(TL - 1, j)

            def weight_lo(c):
                dve.wait_ge(fw_hi_done, c + 1)
                nc.vector.tensor_tensor(fw_lo[:, c, :], bank[WLT_BANK[c]][:, :], fw_hi[:, c, :].bitcast(fp32),
                                        ALU.subtract).then_inc(fw_lo_done, 1)

            def feed_forward(phase_no, gate, b):
                count = B * (phase_no // 2) + b + 1
                dve.wait_ge(fy_ps, count)
                dve.wait_ge(biased, count)
                nc.vector.scalar_tensor_tensor(out=xr[:, b, :], in0=bank[2 + b % 2][:, :], scalar=gate, in1=xr[:, b, :],
                                               op0=ALU.mult, op1=ALU.add).then_inc(facc_done, 1)

            def token_gates(part):
                dve.wait_ge(rstd_done, 4 + part.stop // 2)
                link(nc.vector.tensor_tensor(norm_sq[:, part], mv[:, part, 1], rstd[:, part], ALU.mult))
                link(nc.vector.tensor_tensor(norm_sq[:, part], norm_sq[:, part], rstd[:, part], ALU.mult))
                link(nc.vector.tensor_scalar(gate_hi[:, part], norm_sq[:, part], float(D), EST_T ** 2, ALU.mult, ALU.is_gt))
                link(nc.vector.tensor_scalar(gate_lo[:, part], gate_hi[:, part], -1.0, 1.0, ALU.mult, ALU.add))
                if part.stop == B:
                    nc.vector.tensor_reduce(any_hi[:, 0:1], gate_hi[:, :], axis=AX.X, op=ALU.max).then_inc(any_done, 1)
                    dve.wait_ge(any_done, 1)
                    link(nc.vector.tensor_scalar(gate_hi[:, :], gate_hi[:, :], tg[:, 2:3], None, ALU.mult))
                link(nc.vector.tensor_scalar(gate_lo[:, part], gate_lo[:, part], tg[:, 2:3], None, ALU.mult))

            def low_forward(b):
                feed_forward(1, gate_lo[:, b:b + 1], b)

            maxima(U, (BODY - 1) % 2)
            weight_lo(0)
            weight_lo(1)
            inverse_sums(U, B - 2)
            dve.wait_ge(acc_done, U - 3)
            row_stats(1, 0)
            probabilities_out(U)
            accumulate(U - 2, 2)
            normed_rows(1, 0)
            normed_rows(1, 1)
            weight_lo(2)
            weight_lo(3)
            output_lo(U, (BODY - 1) % 2)
            dve.wait_ge(acc_done, U - 2)
            row_stats(1, 1)
            accumulate(U - 1, 4)
            transposed_lo(1, 0)
            transposed_lo(1, 1)
            normed_rows(1, 2)
            normed_rows(1, 3)
            dve.wait_ge(acc_done, U - 1)
            row_stats(1, 2)
            token_gates(slice(0, 4))
            accumulate(U, 6)
            dve.wait_ge(acc_done, U)
            row_stats(1, 3)
            transposed_lo(1, 2)
            transposed_lo(1, 3)
            normed_rows(1, 4)
            normed_rows(1, 5)
            low_forward(0)
            token_gates(slice(4, B))
            transposed_lo(1, 4)
            low_forward(1)
            transposed_lo(1, 5)
            normed_rows(1, 6)
            normed_rows(1, 7)
            dve.wait_ge(all_done, 1)
            nc.vector.tensor_copy(flag[:, :], any_hi[:, 1:2]).then_inc(flag_done, 1)
            low_forward(2)
            transposed_lo(1, 6)
            transposed_lo(1, 7)
            low_forward(3)

            with dve.If(some_high(dve)):
                high_steps = [0]

                def high_link(op):
                    high_steps[0] += 1
                    op.then_inc(hi_chain, 1)
                    dve.wait_ge(hi_chain, high_steps[0])

                dve.wait_ge(hi_in, 32)
                dve.wait_ge(biased, B)
                dve.wait_ge(facc_done, 4)
                high_link(nc.vector.memset(idx8[:, :, :], 0))
                high_link(nc.vector.memset(code_now[:, :], 0.0))
                for plane in range(HI_BITS):
                    unpack(plane, "shift mask add", qw8, wl8[:, :, :].bitcast(i32), idx8, high_link)
                nc.vector.memset(wl8[:, :, :], 0.0).then_inc(hi_add, 1)
                first_code = high_steps[0]
                with dve.Fori(0, 2 ** HI_BITS) as code:
                    for c in range(C):
                        dve.wait_ge(hi_add, C * code + c + 1)
                        nc.vector.tensor_scalar(eq8[:, :], idx8[:, c, :], code_now[:, :], lut8_sb[:, c, bass.ds(code, 1)],
                                                ALU.is_equal, ALU.mult).then_inc(hi_eq, 1)
                        dve.wait_ge(hi_eq, C * code + c + 1)
                        nc.vector.tensor_tensor(wl8[:, c, :], wl8[:, c, :], eq8[:, :], ALU.add).then_inc(hi_add, 1)
                    nc.vector.tensor_scalar(code_now[:, :], code_now[:, :], 1.0, None, ALU.add).then_inc(hi_chain, 1)
                    dve.wait_ge(hi_chain, code + first_code + 1)
                for c in range(C):
                    dve.wait_ge(hi_fw_hi, c + 1)
                    nc.vector.tensor_tensor(fw8_lo[:, c, :], bank[4 + c][:, :], fw8_hi[:, c, :].bitcast(fp32),
                                            ALU.subtract).then_inc(hi_fw_lo, 1)
                for b in range(B):
                    dve.wait_ge(hi_y, b + 1)
                    nc.vector.scalar_tensor_tensor(out=xr[:, b, :], in0=bank[2 + b % 2][:, :], scalar=gate_hi[:, b:b + 1],
                                                   in1=xr[:, b, :], op0=ALU.mult, op1=ALU.add).then_inc(hi_acc, 1)
                dve.wait_ge(hi_acc, B)

            dve.wait_ge(facc_done, 2)
            row_stats(2, 0)
            low_forward(4)
            normed_rows(2, 0)
            normed_rows(2, 1)
            low_forward(5)
            dve.wait_ge(facc_done, 4)
            row_stats(2, 1)
            transposed_lo(2, 0)
            low_forward(6)
            transposed_lo(2, 1)
            normed_rows(2, 2)
            normed_rows(2, 3)
            low_forward(7)
            dve.wait_ge(facc_done, 6)
            row_stats(2, 2)
            dve.wait_ge(facc_done, B)
            row_stats(2, 3)

            def split_hi(n, piece, parity):
                dve.wait_ge(w1_in[piece], 16 * n)
                cols = slice(1024 * piece, 1024 * (piece + 1))
                nc.vector.tensor_scalar(w1_hi[:, parity, cols], stage1[:, piece % 2, :], 1.0, None,
                                        ALU.mult).then_inc(w1_hi_done[piece], 1)

            def split_lo(n, piece, parity):
                dve.wait_ge(w1_hi_done[piece], n)
                cols = slice(1024 * piece, 1024 * (piece + 1))
                nc.vector.tensor_tensor(w1_lo[:, parity, cols], stage1[:, piece % 2, :],
                                        w1_hi[:, parity, cols].bitcast(fp32), ALU.subtract).then_inc(w1_lo_done[piece], 1)

            def k_mean(count):
                dve.wait_ge(ksq1, count)
                nc.vector.tensor_scalar(k_ms[:, :], k_ss[:, :], 1.0 / P, EPS_QK, ALU.mult, ALU.add).then_inc(kms1, 1)

            def v_low(count, place):
                dve.wait_ge(ksq1, count)
                nc.vector.tensor_tensor(v_lo[:, place, :, :], by2(KVB[:, :])[:, :, P:2 * P],
                                        v_hi[:, place, :, :].bitcast(fp32), ALU.subtract).then_inc(vl1, 1)

            def k_scaled(count):
                dve.wait_ge(kr1, count)
                for tile in range(2):
                    last_op = nc.vector.tensor_scalar(k_sb[:, tile, :], by2(KVB[:, :])[:, tile, 0:P],
                                                      k_r[:, tile:tile + 1], None, ALU.mult)
                last_op.then_inc(ks1, 1)

            def q_mean(count):
                dve.wait_ge(qsq1, count)
                nc.vector.tensor_reduce(q_ss[:, :], by4(q_sq[:, :]), axis=AX.X, op=ALU.add).then_inc(qss1, 1)
                dve.wait_ge(qss1, count)
                nc.vector.tensor_scalar(q_ms[:, :], q_ss[:, :], 1.0, EPS_QK * P, ALU.mult, ALU.add).then_inc(qms1, 1)

            v_low(1, 0)
            k_mean(1)
            normed_rows(2, 4)
            normed_rows(2, 5)
            k_scaled(1)
            q_mean(1)

            def maxima1(count, parity):
                dve.wait_ge(s1, count)
                wait(dve, e1, count - 1)
                for a in range(2):
                    last_op = nc.vector.tensor_reduce(nmax1[:, 2 * a:2 * a + 2], by2((S0B, S1B)[a][:, :]),
                                                      axis=AX.X, op=ALU.max, negate=True)
                last_op.then_inc(nm1, 1)
                dve.wait_ge(nm1, count)
                dve.wait_ge(qr1, count)
                nc.vector.tensor_tensor(nb1[:, :], nmax1[:, :], q_r[:, parity, :], ALU.mult).then_inc(nb1s, 1)

            def inverse_sums1(count):
                dve.wait_ge(e1, count)
                nc.vector.reciprocal(rn1[:, :], sum1[:, :]).then_inc(rn1s, 1)

            def accumulate1(count, b):
                dve.wait_ge(y1, count)
                nc.vector.scalar_tensor_tensor(out=xr[:, b, :], in0=Y1B[:, :], scalar=tg[:, 1:2], in1=xr[:, b, :],
                                               op0=ALU.mult, op1=ALU.add).then_inc(acc1, 1)

            def probabilities_lo(count):
                dve.wait_ge(ph1, count)
                for kc in range(2):
                    last_op = nc.vector.tensor_tensor(pt_lo[:, kc, :], (T0B, T1B)[kc][:, :],
                                                      pt_hi[:, kc, :].bitcast(fp32), ALU.subtract)
                last_op.then_inc(pl1, 1)

            def output1_lo(count):
                dve.wait_ge(oh1, count)
                nc.vector.tensor_tensor(ot1_lo[:, :], O1B[:, :], ot1_hi[:, :].bitcast(fp32),
                                        ALU.subtract).then_inc(ol1, 1)

            def slot1(t, j):
                i = BODY * t + j
                first = isinstance(t, int) and t == 0
                last = isinstance(t, int) and t == TL - 1
                lag1 = not (first and j < 1)
                ahead = not (last and j == BODY - 1)
                if lag1 and not (first and j == 1):
                    maxima1(i, (j - 1) % 2)
                dve.wait_ge(qh1, i + 1)
                nc.vector.tensor_tensor(qt_lo[:, :], Q1B[:, :], qt_hi[:, :].bitcast(fp32), ALU.subtract).then_inc(ql1, 1)
                dve.wait_ge(kh1, i + 1)
                nc.vector.scalar_tensor_tensor(out=kt_lo[:, :], in0=KVB[:, 0:256], scalar=kw[:, 0:1],
                                               in1=kt_hi[:, :].bitcast(fp32), op0=ALU.mult,
                                               op1=ALU.subtract).then_inc(kl1, 1)
                if first and j == 0:
                    transposed_lo(2, 2)
                    transposed_lo(2, 3)
                    normed_rows(2, 6)
                    normed_rows(2, 7)
                if first and j == 1:
                    maxima1(i, 0)
                    transposed_lo(2, 6)
                    transposed_lo(2, 7)
                if not last and 1 <= j < 6:
                    split_lo(t + 1, j - 1, (t + 1) % 2)
                if lag1:
                    inverse_sums1(i)
                if not (first and j < 2):
                    accumulate1(i - 1, (j - 2) % B)
                if last and j in (3, 5, 7):
                    dve.wait_ge(acc1, i - 1)
                    row_stats(3, (j - 3) // 2)
                if last and j == 2:
                    dve.wait_ge(fbias_in, 32)
                    nc.vector.tensor_scalar(fbias1, fbias16, tg[:, 3:4], None, ALU.mult)
                if last and j in (4, 6):
                    normed_rows(3, j - 4)
                    normed_rows(3, j - 3)
                if ahead:
                    v_low(i + 2, (j + 1) % 4)
                    k_mean(i + 2)
                if first and j == 0:
                    transposed_lo(2, 4)
                    transposed_lo(2, 5)
                if not last and j < 5:
                    wait(dve, y1 if j >= 3 else q1, 8 * t)
                    split_hi(t + 1, j, (t + 1) % 2)
                if lag1:
                    probabilities_lo(i)
                if ahead:
                    k_scaled(i + 2)
                    q_mean(i + 2)
                if lag1:
                    output1_lo(i)
            for j in range(BODY):
                slot1(0, j)
            with dve.Fori(1, TL - 1) as t:
                for j in range(BODY):
                    slot1(t, j)
            for j in range(BODY):
                slot1(TL - 1, j)

            maxima1(U, (BODY - 1) % 2)
            transposed_lo(3, 0)
            transposed_lo(3, 1)
            inverse_sums1(U)
            normed_rows(3, 4)
            normed_rows(3, 5)
            accumulate1(U - 1, 6)
            probabilities_lo(U)
            transposed_lo(3, 2)
            feed_forward(3, tg[:, 3:4], 0)
            transposed_lo(3, 3)
            feed_forward(3, tg[:, 3:4], 1)
            output1_lo(U)
            accumulate1(U, 7)
            dve.wait_ge(acc1, U)
            row_stats(3, 3)
            transposed_lo(3, 4)
            feed_forward(3, tg[:, 3:4], 2)
            transposed_lo(3, 5)
            normed_rows(3, 6)
            normed_rows(3, 7)
            feed_forward(3, tg[:, 3:4], 3)
            transposed_lo(3, 6)
            transposed_lo(3, 7)
            for b in range(4, B):
                feed_forward(3, tg[:, 3:4], b)

        @block.tensor
        def _(pe):
            def passes(out_ap, terms):
                n = len(terms)
                for c, (l_hi, l_lo, r_hi, r_lo) in enumerate(terms):
                    nc.tensor.matmul(out_ap, l_hi, r_hi, start=(c == 0), stop=False)
                    nc.tensor.matmul(out_ap, l_hi, r_lo, start=False, stop=False)
                    op = nc.tensor.matmul(out_ap, l_lo, r_hi, start=False, stop=(c == n - 1))
                return op

            def transpose_rows(phase_no, b):
                count = B * phase_no + b + 1
                pe.wait_ge(*((z0_done, count) if phase_no == 0 else (z_done, count - B)))
                if phase_no in (1, 3) or b >= 4:
                    pe.wait_ge(xt_lo_done, count - (4 if phase_no in (0, 2) else 2))
                place = z_rows(phase_no, b)
                for c in range(C):
                    op = nc.tensor.transpose(bank[XT_BANK[phase_no][b]][:, tok(c)], place[:, tok(c)], ident[:, :])
                op.then_inc(xt_ps, 1)

            pe.wait_ge(ident_done, 2)

            def transposed_probabilities(count):
                pe.wait_ge(norm_done, count)
                wait(pe, pt_done, count - 1)
                for a in range(4):
                    op = nc.tensor.transpose(by4(TB[:, :])[:, a, :], by4(pr)[:, a, :], ident[:, :])
                op.then_inc(pt_ps, 1)

            def attention_output(count, parity):
                pe.wait_ge(pt_done, count)
                pe.wait_ge(v_done, count)
                wait(pe, ot_lo_done, count - 1)
                for h in range(2):
                    for bb in range(2):
                        a = 2 * h + bb
                        v = vs[:, parity, 256 * bb + P * h:256 * bb + P * (h + 1)]
                        op = nc.tensor.matmul(by4(OB[:, :])[:, a, :], v, by4(ptr)[:, a, :], start=True, stop=True)
                op.then_inc(o_ps, 1)

            def output_projection(count, k, n):
                if k % 4 == 0:
                    pe.wait_ge(w_lo_done[3], n + 1)
                pe.wait_ge(ot_lo_done, count)
                wait(pe, acc_done, count - 1)
                par = k // 4
                for bb, yb in ((0, YA), (1, YB)):
                    op = passes(yb[:, :], [
                        (by4(ot0_hi[:, k % 2, :])[:, 2 * h + bb, :], by4(ot0_lo[:, k % 2, :])[:, 2 * h + bb, :],
                         w0_hi[:, par, 3, 512 * h:512 * (h + 1)], w0_lo[:, par, 3, 512 * h:512 * (h + 1)])
                        for h in range(2)])
                op.then_inc(y_ps, 1)

            def slot(t, j):
                i, n, p, parity = BODY * t + j, 2 * t + j // 4, j % 4, (j // 4) % 2
                first = isinstance(t, int) and t == 0
                wh, wlo = w0_hi[:, parity, :, :], w0_lo[:, parity, :, :]

                def projected(dst, w, xh, xl, done, free):
                    if p == 0:
                        pe.wait_ge(w_lo_done[w], n + 1)
                    if first and p == j:
                        pe.wait_ge(*((xt_lo_done, 2 * j + 2) if w == 0 else (ctx_lo_done, j + 1)))
                    wait(pe, free, i)
                    tokens = slice(2 * p * P, 2 * (p + 1) * P)
                    for h in range(2):
                        cols = lambda a, c: a[:, w, 256 * c + P * h:256 * c + P * (h + 1)]
                        op = passes(by2(dst[:, :])[:, h, :],
                                    [(cols(wh, c), cols(wlo, c), xh[:, c, tokens], xl[:, c, tokens]) for c in range(C)])
                    op.then_inc(done, 1)

                def values():
                    if p == 0:
                        pe.wait_ge(w_lo_done[2], n + 1)
                    wait(pe, v_done, i)
                    for bb in range(2):
                        b = 2 * p + bb
                        op = passes(by2(VB[:, :])[:, bb, :],
                                    [(ct_hi[:, c, tok(b)], ct_lo[:, c, tok(b)], wh[:, 2, 256 * c:256 * (c + 1)],
                                      wlo[:, 2, 256 * c:256 * (c + 1)]) for c in range(C)])
                    op.then_inc(v_ps, 1)

                if first and j == 0:
                    projected(KB, 1, ct_hi, ct_lo, k_ps, kt_done)
                    values()
                    transpose_rows(0, 0)
                    transpose_rows(0, 1)
                    projected(QB, 0, xt_hi, xt_lo, q_ps, qt_done)
                    transpose_rows(0, 2)
                    transpose_rows(0, 3)
                else:
                    if first and j == 1:
                        transpose_rows(0, 4)
                        transpose_rows(0, 5)
                    projected(QB, 0, xt_hi, xt_lo, q_ps, qt_done)
                    projected(KB, 1, ct_hi, ct_lo, k_ps, kt_done)
                    if first and j == 1:
                        pe.wait_ge(xt_lo_done, 6)
                    transposed_probabilities(i)
                    values()
                    attention_output(i, (j - 1) % 2)
                if not (first and j < 2):
                    if first and j == 2:
                        pe.wait_ge(xt_lo_done, B)
                    output_projection(i - 1, (j - 2) % BODY, 2 * t + (j - 2) // 4)
                if first and j == 1:
                    transpose_rows(0, 6)
                    transpose_rows(0, 7)
                pe.wait_ge(qt_done, i + 1)
                pe.wait_ge(kt_done, i + 1)
                wait(pe, added, i)
                for h in range(2):
                    for bb in range(2):
                        part = slice(256 * h + P * bb, 256 * h + P * (bb + 1))
                        op = nc.tensor.matmul(SB[:, part], qt[:, part], kt[:, part], start=True, stop=True)
                op.then_inc(s_ps, 1)

            for j in range(BODY):
                slot(0, j)
            with pe.Fori(1, TL - 1) as t:
                for j in range(BODY):
                    slot(t, j)
            for j in range(BODY):
                slot(TL - 1, j)

            def transpose_weight(c):
                if c < 3:
                    pe.wait_ge((qt_done, kt_done, v_done)[c], U)
                else:
                    pe.wait_ge(fw_lo_done, 1)
                for o in range(C):
                    op = nc.tensor.transpose(bank[WLT_BANK[c]][:, tok(o)], wl[:, o, tok(c)], ident[:, :])
                op.then_inc(wlt_ps, 1)

            def ffn(phase_no, b, terms):
                count = B * (phase_no // 2) + b + 1
                pe.wait_ge(xt_lo_done, B * phase_no + b + 1)
                if b >= 2:
                    pe.wait_ge(facc_done, count - 2)
                n = len(terms)
                for k, (x_part, w_part, c) in enumerate(terms):
                    op = nc.tensor.matmul(bank[2 + b % 2][:, :], x_part[:, c, tok(b)], w_part[:, c, :],
                                          start=(k == 0), stop=(k == n - 1))
                op.then_inc(fy_ps, 1)

            def low_ffn(b):
                ffn(1, b, [(x_part, w_part, c) for c in range(C)
                           for x_part, w_part in ((xt_hi, fw_hi), (xt_hi, fw_lo), (xt_lo, fw_hi))])

            def last_ffn(b):
                ffn(3, b, [(x_part, fw1, c) for c in range(C) for x_part in (xt_hi, xt_lo)])

            pe.wait_ge(wl_done, C * 2 ** LO_BITS)
            for c in range(C):
                transpose_weight(c)
            transposed_probabilities(U)
            attention_output(U, (BODY - 1) % 2)
            output_projection(U - 1, BODY - 2, NG - 1)
            pe.wait_ge(fw_lo_done, C)
            transpose_rows(1, 0)
            transpose_rows(1, 1)
            output_projection(U, BODY - 1, NG - 1)
            transpose_rows(1, 2)
            transpose_rows(1, 3)
            pe.wait_ge(added, U)
            low_ffn(0)
            low_ffn(1)
            transpose_rows(1, 4)
            transpose_rows(1, 5)
            low_ffn(2)
            transpose_rows(1, 6)
            transpose_rows(1, 7)
            low_ffn(3)
            with pe.If(some_high(pe)):
                pe.wait_ge(hi_add, C * 2 ** HI_BITS + 1)
                pe.wait_ge(acc_done, U)
                pe.wait_ge(ot_lo_done, U)
                for c in range(C):
                    for o in range(C):
                        op = nc.tensor.transpose(bank[4 + c][:, tok(o)], wl8[:, o, tok(c)], ident[:, :])
                    op.then_inc(hi_wt, 1)
                pe.wait_ge(hi_fw_lo, C)
                pe.wait_ge(facc_done, 4)
                pe.wait_ge(xt_lo_done, 2 * B)
                for b in range(B):
                    wait(pe, hi_acc, b - 1)
                    op = passes(bank[2 + b % 2][:, :], [(xt_hi[:, c, tok(b)], xt_lo[:, c, tok(b)], fw8_hi[:, c, :],
                                                         fw8_lo[:, c, :]) for c in range(C)])
                    op.then_inc(hi_y, 1)
                pe.wait_ge(hi_acc, B)
            low_ffn(4)
            low_ffn(5)
            transpose_rows(2, 0)
            low_ffn(6)
            transpose_rows(2, 1)
            low_ffn(7)
            def keys_values(b, parity, count):
                wait(pe, kl1, count - 1)
                wait(pe, vl1, count - 1)
                for tile, (xh, xl) in enumerate(((ct_hi, ct_lo), (xt_hi, xt_lo))):
                    op = passes(by2(KVB[:, :])[:, tile, :],
                                [(xh[:, c, tok(b)], xl[:, c, tok(b)], w1_hi[:, parity, 256 * c:256 * (c + 1)],
                                  w1_lo[:, parity, 256 * c:256 * (c + 1)]) for c in range(C)])
                op.then_inc(kv1, 1)

            def queries(b, parity, count):
                wait(pe, ql1, count - 1)
                op = passes(Q1B[:, :], [(xt_hi[:, c, tok(b)], xt_lo[:, c, tok(b)],
                                         w1_hi[:, parity, 1024 + 512 * c:1024 + 512 * (c + 1)],
                                         w1_lo[:, parity, 1024 + 512 * c:1024 + 512 * (c + 1)]) for c in range(C)])
                op.then_inc(q1, 1)

            pe.wait_ge(first_lo, 5)
            pe.wait_ge(xt_lo_done, 2 * B + 1)
            keys_values(0, 0, 1)
            queries(0, 0, 1)
            transpose_rows(2, 2)
            transpose_rows(2, 3)

            def output_projection1(count, par):
                pe.wait_ge(ol1, count)
                wait(pe, acc1, count - 1)
                op = passes(Y1B[:, :], [(ot1_hi[:, tok(h)], ot1_lo[:, tok(h)],
                                         w1_hi[:, par, 3072 + 512 * h:3072 + 512 * (h + 1)],
                                         w1_lo[:, par, 3072 + 512 * h:3072 + 512 * (h + 1)]) for h in range(GQ)])
                op.then_inc(y1, 1)

            def transposed_probabilities1(count):
                wait(pe, pl1, count - 1)
                for half_p, ready in ((0, pn1a), (2, pn1b)):
                    pe.wait_ge(ready, count)
                    for a in range(half_p, half_p + 2):
                        for kc in range(2):
                            op = nc.tensor.transpose(by4((T0B, T1B)[kc][:, :])[:, a, :], p1[:, a, tok(kc)], ident[:, :])
                op.then_inc(d1, 1)

            def attention_output1(count, place):
                pe.wait_ge(pl1, count)
                wait(pe, ol1, count - 1)
                op = passes(O1B[:, :], [(v_hi[:, place, kc, :], v_lo[:, place, kc, :], pt_hi[:, kc, :], pt_lo[:, kc, :])
                                        for kc in range(2)])
                op.then_inc(o1, 1)

            def slot1(t, j):
                i = BODY * t + j
                first = isinstance(t, int) and t == 0
                last = isinstance(t, int) and t == TL - 1
                ahead = not (last and j == BODY - 1)
                own, other = t % 2, (t + 1) % 2
                pe.wait_ge(qc1, i + 1)
                pe.wait_ge(qsq1, i + 1)
                for a in range(4):
                    op = nc.tensor.transpose(by4(Q1B[:, :])[:, a, :], by4(q_sb[:, :])[:, a, :], ident[:, :])
                op.then_inc(tq1, 1)
                pe.wait_ge(ks1, i + 1)
                pe.wait_ge(vl1, i + 1)
                for a in range(2):
                    op = nc.tensor.transpose(KVB[:, tok(a)], k_sb[:, a, :], ident[:, :])
                op.then_inc(tk1, 1)
                if not (first and j < 2):
                    output_projection1(i - 1, own if j >= 2 else other)
                if ahead:
                    if j == BODY - 1:
                        for piece in range(5):
                            pe.wait_ge(w1_lo_done[piece], t + 1)
                    if first:
                        pe.wait_ge(xt_lo_done, 2 * B + j + 2 if j < BODY - 1 else 3 * B)
                    keys_values((j + 1) % B, other if j == BODY - 1 else own, i + 2)
                if first and j == 0:
                    transpose_rows(2, 4)
                    transpose_rows(2, 5)
                if not (first and j < 1):
                    if first and j == 1:
                        pe.wait_ge(xt_lo_done, 3 * B)
                    transposed_probabilities1(i)
                if ahead:
                    queries((j + 1) % B, other if j == BODY - 1 else own, i + 2)
                if not (first and j < 1):
                    attention_output1(i, (j - 1) % 4)
                if first and j == 0:
                    transpose_rows(2, 6)
                    transpose_rows(2, 7)
                    pe.wait_ge(facc_done, B)
                pe.wait_ge(ql1, i + 1)
                pe.wait_ge(kl1, i + 1)
                wait(pe, e1, i)
                for a in range(4):
                    op = passes(by2((S0B, S1B)[a // 2][:, :])[:, a % 2, :],
                                [(qt_hi[:, tok(a)], qt_lo[:, tok(a)], kt_hi[:, :], kt_lo[:, :])])
                op.then_inc(s1, 1)

            for j in range(BODY):
                slot1(0, j)
            with pe.Fori(1, TL - 1) as t:
                for j in range(BODY):
                    slot1(t, j)
            for j in range(BODY):
                slot1(TL - 1, j)

            output_projection1(U - 1, (KV - 1) % 2)
            transpose_rows(3, 0)
            transpose_rows(3, 1)
            pe.wait_ge(fw_hi_done, 2 * C)
            pe.wait_ge(e1, U)
            last_ffn(0)
            transposed_probabilities1(U)
            last_ffn(1)
            transpose_rows(3, 2)
            transpose_rows(3, 3)
            attention_output1(U, (BODY - 1) % 4)
            last_ffn(2)
            output_projection1(U, (KV - 1) % 2)
            transpose_rows(3, 4)
            last_ffn(3)
            transpose_rows(3, 5)
            last_ffn(4)
            last_ffn(5)
            transpose_rows(3, 6)
            transpose_rows(3, 7)
            last_ffn(6)
            last_ffn(7)


def kernel(**inputs):
    import numpy as np
    import concourse.bacc as bacc
    from concourse.bass_utils import run_bass_kernel_spmd

    a = {k: np.asarray(v) for k, v in inputs.items()}

    def rows(w, groups):
        return w.reshape(C, P, groups, -1).transpose(2, 1, 0, 3)

    gates = np.concatenate([a["g_xattn"], a["g_ffn"]]).reshape(1, 4)
    qkv0 = [rows(a[f"L0_xattn_w_{n}"].T, NG).reshape(NG, P, 1024) for n in "qkv"]
    out0 = a["L0_xattn_w_out"].T.reshape(NG, 2, P, D).transpose(0, 2, 1, 3).reshape(NG, P, 1024)
    w0 = np.stack([*qkv0, out0], axis=1)
    kv1 = np.concatenate([rows(a["L1_xattn_Wk"], KV), rows(a["L1_xattn_Wv"], KV)], axis=3).reshape(KV, P, 1, 1024)
    q1 = rows(a["L1_xattn_Wq"], KV).reshape(KV, P, 2, 1024)
    o1 = a["L1_xattn_Wo"].reshape(KV, GQ, P, D).transpose(0, 2, 1, 3).reshape(KV, P, 2, 1024)
    w1 = np.concatenate([kv1, q1, o1], axis=2).transpose(0, 2, 1, 3)
    table = lambda t: t.reshape(C, P, -1).transpose(1, 0, 2)
    data = {
        "x": a["x"],
        "ctx_t": a["ctx_4096"].reshape(B * P, C, P).transpose(2, 1, 0),
        "mask": a["mask_BxSxS2_bk0"].view(np.uint8).transpose(1, 0, 2).copy().reshape(P, B * P).view(np.int32),
        "gates": gates,
        "w0": w0,
        "bias0": a["L0_xattn_position_bias"].reshape(NG, 2, P, P).transpose(0, 2, 1, 3).reshape(NG, P, 2 * P),
        "lnw": a["L0_xattn_ln_weight"].reshape(1, D),
        "qweight": a["L0_ffn_qweight"].reshape(HI_BITS, C, P, D // 32).transpose(2, 0, 1, 3).reshape(P, HI_BITS, C * D // 32),
        "lut4": table(a["L0_ffn_lut4"]),
        "lut8": table(a["L0_ffn_lut8"]),
        "ffn0_bias": a["L0_ffn_bias"].reshape(1, D),
        "w1": w1,
        "qk_norm": np.stack([a["L1_xattn_q_norm_w"], a["L1_xattn_k_norm_w"]], axis=1),
        "ffn1_w": a["L1_ffn_weight"].T.reshape(C, P, D).transpose(1, 0, 2).reshape(P, C * D),
        "ffn1_bias": a["L1_ffn_bias"].reshape(1, D),
    }
    data = {k: np.ascontiguousarray(v) for k, v in data.items()}
    nc = bacc.Bacc("TRN2", target_bir_lowering=False, num_devices=1)
    args = [nc.dram_tensor(k, v.shape, mybir.dt.from_np(v.dtype), kind="ExternalInput").ap() for k, v in data.items()]
    args.append(nc.dram_tensor("out", (B, P, D), fp32, kind="ExternalOutput").ap())
    build(nc, *args)
    r = run_bass_kernel_spmd(nc, [data], core_ids=[0])
    return r.results[0]["out"]
```

```python
import concourse.bass as bass
from concourse import mybir
from contextlib import ExitStack

fp32 = mybir.dt.float32
fp32r = mybir.dt.float32r
fp16 = mybir.dt.float16
bf16 = mybir.dt.bfloat16
i32 = mybir.dt.int32
u8 = mybir.dt.uint8
ALU = mybir.AluOpType
ACT = mybir.ActivationFunctionType
AX = mybir.AxisListType

P = 128
B = 8
D = 512
C = D // P
H = 32
KV = 8
GQ = H // KV
NG = H // 2
U = 64
FIRST_ORDER = (2, 3, 4, 0, 1)
BODY = 8
TL = U // BODY
LO_BITS, HI_BITS = 4, 8
EST_T = 64.0
EPS_LN, EPS_RMS, EPS_QK = 1e-5, 1e-5, 1e-6
NEG = 1e30
W1 = 5 * 1024


def wait(eng, sem, count):
    if not (isinstance(count, int) and count < 1):
        eng.wait_ge(sem, count)


def build(nc, x, ctx_t, mask, gates, w0, bias0, lnw, qweight, lut4, lut8, ffn0_bias, w1, qk_norm, ffn1_w, ffn1_bias, out):
    stack = ExitStack()
    with stack:
        def sems(names):
            return [stack.enter_context(nc.semaphore(n)) for n in names.split()]

        def keep(name, shape, dt):
            return stack.enter_context(nc.sbuf_tensor(name, shape, dt))

        xr = keep("residual", [P, B, D], fp32)
        xt_hi = keep("xt_hi", [P, C, B * P], fp32r)
        xt_lo = keep("xt_lo", [P, C, B * P], fp32r)
        ct_hi = keep("ct_hi", [P, C, B * P], fp32r)
        ct_lo = keep("ct_lo", [P, C, B * P], fp32r)
        ident = keep("ident", [P, P], fp32)
        fbias = keep("fbias", [P, D], fp32)
        tg = keep("tg", [P, 4], fp32)
        stats = keep("stats", [P, B, 6], fp32)
        mv = keep("mv", [P, B, 2], fp32)
        ve = keep("ve", [P, 2, B], fp32)
        roots = keep("roots", [P, 2, B], fp32)
        rstd, scale0 = roots[:, 0, :], roots[:, 1, :]
        half = keep("half", [P, B], fp32)
        base_s = keep("base_s", [P, B], fp32)
        base_b = keep("base_b", [P, B], fp32)
        qk_w = keep("qk_w", [P, 2], fp32)
        kw = keep("kw", [P, 1], fp32)
        lut = keep("lut", [P, C, 2 ** LO_BITS], fp32)
        codes = keep("codes", [P, 2 ** LO_BITS], fp32)
        shifts = keep("shifts", [P, 32], i32)
        code_now = keep("code_now", [P, 1], fp32)
        norm_sq = keep("norm_sq", [P, B], fp32)
        gate_hi = keep("gate_hi", [P, B], fp32)
        gate_lo = keep("gate_lo", [P, B], fp32)
        any_hi = keep("any_hi", [P, 2], fp32)
        flag = keep("flag", [P, 1], i32)

        phase = ExitStack()

        def tmp(name, shape, dt):
            return phase.enter_context(nc.sbuf_tensor(name, shape, dt))

        wl = tmp("wl", [P, C, D], fp32)
        w0_hi = tmp("w0_hi", [P, 2, 4, 1024], fp32r)
        w0_lo = tmp("w0_lo", [P, 2, 4, 1024], fp32r)
        stage0 = tmp("stage0", [P, 4, 1024], fp32)
        work = tmp("work", [P, 4608], fp32)
        ot0_hi = tmp("ot0_hi", [P, 2, 512], fp32r)
        ot0_lo = tmp("ot0_lo", [P, 2, 512], fp32r)
        negm = tmp("negm", [P, B, P], bf16)
        valid = tmp("valid", [P, B], fp32)
        bias_sb = tmp("bias_sb", [P, 2, 2 * P], fp32)
        eq = tmp("eq", [P, D], fp32)
        idx = tmp("idx", [P, C, D], u8)
        qw = tmp("qw", [P, LO_BITS, C * D // 32], i32)
        nmax = tmp("nmax", [P, 4], fp32)
        ssum = tmp("ssum", [P, 4], fp32)
        rn = tmp("rn", [P, 4], fp32)
        qt, kt = work[:, 0:512], work[:, 512:1024]
        vs = work[:, 1024:2048].rearrange("p (u n) -> p u n", u=2)
        bm = work[:, 2048:3072].rearrange("p (u n) -> p u n", u=2)
        sc, pr, ptr = work[:, 3072:3584], work[:, 3584:4096], work[:, 4096:4608]
        lnw_bc = wl[:, 0, :]
        z0 = [wl[:, 1, :], wl[:, 2, :], wl[:, 3, :]]
        unpacked = wl[:, :, :].bitcast(i32)
        mask_raw = eq[:, :].bitcast(u8)[:, 0:B * P]
        phase.close()

        phase = ExitStack()
        w1_hi = tmp("w1_hi", [P, 2, W1], fp32r)
        w1_lo = tmp("w1_lo", [P, 2, W1], fp32r)
        ot1_hi = tmp("ot1_hi", [P, 512], fp32r)
        ot1_lo = tmp("ot1_lo", [P, 512], fp32r)
        pt_hi = tmp("pt_hi", [P, 2, 512], fp32r)
        pt_lo = tmp("pt_lo", [P, 2, 512], fp32r)
        qt_hi = tmp("qt_hi", [P, 512], fp32r)
        qt_lo = tmp("qt_lo", [P, 512], fp32r)
        kt_hi = tmp("kt_hi", [P, 256], fp32r)
        kt_lo = tmp("kt_lo", [P, 256], fp32r)
        v_hi = tmp("v_hi", [P, 4, 2, P], fp32r)
        v_lo = tmp("v_lo", [P, 4, 2, P], fp32r)
        stage1 = tmp("stage1", [P, 2, 1024], fp32)
        q_sb = tmp("q_sb", [P, 512], fp32)
        q_sq = tmp("q_sq", [P, 512], fp32)
        k_sb = fbias[:, 0:256].rearrange("p (a n) -> p a n", a=2)
        k_sq = fbias[:, 256:512].rearrange("p (a n) -> p a n", a=2)
        p1 = tmp("p1", [P, 4, 256], fp32)
        k_ss = tmp("k_ss", [P, 2], fp32)
        k_ms = tmp("k_ms", [P, 2], fp32)
        k_r = tmp("k_r", [P, 2], fp32)
        q_ss = tmp("q_ss", [P, 4], fp32)
        q_ms = tmp("q_ms", [P, 4], fp32)
        q_r = tmp("q_r", [P, 2, 4], fp32)
        nmax1 = tmp("nmax1", [P, 4], fp32)
        nb1 = tmp("nb1", [P, 4], fp32)
        sum1 = tmp("sum1", [P, 4], fp32)
        rn1 = tmp("rn1", [P, 4], fp32)
        fbias16 = stage1[:, :, :].bitcast(fp16)[:, 1, 0:D]
        phase.close()

        phase = ExitStack()
        tmp("below_second_low_weights", [P, C * D + 8 * 1024 + 4 * 1024], fp32)
        ctx_stage = tmp("ctx_stage", [P, B // 2, C * 2 * P], fp32)
        ctx_raw = [ctx_stage[:, p, :].rearrange("p (c n) -> p c n", c=C) for p in range(B // 2)]
        phase.close()

        phase = ExitStack()
        tmp("high_weights_of_layer_1", [P, 2 * W1], fp32)
        plain1 = tmp("plain1", [P, W1], fp32)
        phase.close()

        phase = ExitStack()
        tmp("weights_of_layer_1", [P, 2 * 2 * W1], fp32)
        z_mid = tmp("z_mid", [P, 4, D], fp32)
        wl8 = tmp("wl8", [P, C, D], fp32)
        eq8 = tmp("eq8", [P, D], fp32)
        idx8 = tmp("idx8", [P, C, D], u8)
        qw8 = tmp("qw8", [P, HI_BITS, C * D // 32], i32)
        lut8_sb = tmp("lut8_sb", [P, C, 2 ** HI_BITS], fp32)
        phase.close()
        by_chunk = lambda ap: ap.rearrange("p (c n) -> p c n", c=C)
        fw_hi, fw_lo = by_chunk(w1_hi[:, 1, 0:2048]), by_chunk(w1_lo[:, 1, 0:2048])
        fw8_hi, fw8_lo = by_chunk(w1_hi[:, 1, 2048:4096]), by_chunk(w1_lo[:, 1, 2048:4096])
        fw1 = by_chunk(w1_hi[:, 0, 0:2048])
        fbias1 = plain1[:, 4096:4096 + D]

        pairs = tuple(slice(b, b + 2) for b in range(0, B, 2))
        PARTS = (pairs, pairs, pairs, pairs[:3] + (slice(6, 7), slice(7, 8)))

        def z_rows(phase_no, b):
            if phase_no == 0:
                return z0[b % 3]
            if phase_no < 3:
                return z_mid[:, b % 4, :]
            return plain1[:, D * b:D * (b + 1)]

        WLT_BANK = (0, 1, 2, 0)
        XT_BANK = ((3, 4, 6, 7, 4, 5, 6, 7), (3, 1, 0, 1, 0, 1, 0, 1), (4, 5, 6, 7) * 2, (0, 0, 1, 0, 1, 0, 1, 0))
        FFN_BANK = {1: (2, 3) * 4, 3: (1, 2, 3, 2, 3, 2, 3, 2)}

        bank = [stack.enter_context(nc.psum_tensor(f"bank{n}", [P, 512], fp32)) for n in range(8)]
        QB, KB, VB, SB, TB, OB, YA, YB = bank
        KVB, Q1B, S0B, S1B, T0B, T1B, O1B, Y1B = bank

        x_in = sems(" ".join(f"x_in{b}" for b in range(B)))
        gate_in, lnw_in, mask_in, quant_in, fbias_in, const_done = sems(
            "gate_in lnw_in mask_in quant_in fbias_in const_done")
        chain, ident_done, half_done = sems("chain ident_done half_done")
        ctx_hi_done, ctx_lo_done, tanh_done, negm_done, valid_done = sems(
            "ctx_hi_done ctx_lo_done tanh_done negm_done valid_done")
        (ve_done, rstd_done, z_done, xt_ps, xt_hi_done, xt_lo_done) = sems(
            "ve_done rstd_done z_done xt_ps xt_hi_done xt_lo_done")
        z0_centred, z0_done = sems("z0_centred z0_done")
        base_ready, base_done, biased = sems("base_ready base_done biased")
        first_in, first_hi, first_lo = sems("first_in first_hi first_lo")
        (q_ps, k_ps, v_ps, s_ps, pt_ps, o_ps, y_ps) = sems("q_ps k_ps v_ps s_ps pt_ps o_ps y_ps")
        (qt_done, kt_done, v_done, exp_done, ot_hi_done) = sems("qt_done kt_done v_done exp_done ot_hi_done")
        (added, max_done, recip_done, rn_done, pt_done, ot_lo_done, acc_done) = sems(
            "added max_done recip_done rn_done pt_done ot_lo_done acc_done")
        (bm_done, norm_done) = sems("bm_done norm_done")
        ctx_in = sems(" ".join(f"ctx_in{p}" for p in range(B // 2)))
        w_in, w_hi_done, w_lo_done = (sems(" ".join(f"{n}{w}" for w in "qkvo")) for n in ("w_in_", "w_hi_", "w_lo_"))
        bias_in = sems("bias_in_even bias_in_odd")
        eq_done, wl_done = sems("eq_done wl_done")
        wlt_ps, fw_hi_done, fw_lo_done, fw_in = sems("wlt_ps fw_hi_done fw_lo_done fw_in")
        fy_ps, facc_done, out_done = sems("fy_ps facc_done out_done")
        w1_in, w1_hi_done, w1_lo_done = (sems(" ".join(f"{n}{w}" for w in range(5))) for n in ("w1_in_", "w1_hi_", "w1_lo_"))
        kv1_ps, q1_ps, kt1_ps, qt1_ps, s1_ps, pt1_ps, o1_ps, y1_ps = sems(
            "kv1_ps q1_ps kt1_ps qt1_ps s1_ps pt1_ps o1_ps y1_ps")
        (k1_squared, q1_copied, q1_squared, qt1_hi_done, kt1_hi_done, exp1_done, pt1_hi_first, pt1_hi_second,
         ot1_hi_done) = sems("k1_squared q1_copied q1_squared qt1_hi_done kt1_hi_done exp1_done pt1_hi_first "
                             "pt1_hi_second ot1_hi_done")
        (v1_lo_done, k1_mean_done, k1_scaled, q1_sum_done, q1_mean_done, qt1_lo_done, kt1_lo_done, max1_done, shift1_done,
         recip1_done, pt1_lo_done, ot1_lo_done, acc1_done) = sems(
            "v1_lo_done k1_mean_done k1_scaled q1_sum_done q1_mean_done qt1_lo_done kt1_lo_done max1_done shift1_done "
            "recip1_done pt1_lo_done ot1_lo_done acc1_done")
        k1_root_done, q1_root_done, norm1_first, norm1_second = sems("k1_root_done q1_root_done norm1_first norm1_second")
        (qk_in,) = sems("qk_in")
        any_done, all_done, flag_done = sems("any_done all_done flag_done")
        hi_in, hi_eq, hi_add, hi_chain, hi_wt, hi_fw_hi, hi_fw_lo, hi_y, hi_acc = sems(
            "hi_in hi_eq hi_add hi_chain hi_wt hi_fw_hi hi_fw_lo hi_y hi_acc")

        block = stack.enter_context(nc.Block())
        tok = lambda b: slice(b * P, (b + 1) * P)
        by4 = lambda ap: ap.rearrange("p (a n) -> p a n", a=4)
        by2 = lambda ap: ap.rearrange("p (a n) -> p a n", a=2)

        def some_high(eng):
            eng.wait_ge(flag_done, 1)
            return eng.value_load(flag[0:1, 0:1], min_val=0, max_val=1)

        @block.sync
        def _(sp):
            sp.dma_start(tg[:, :], gates.to_broadcast([P, 4])).then_inc(gate_in, 16)

            def load_context(p):
                sp.dma_start(ctx_raw[p], ctx_t[:, :, 2 * p * P:2 * (p + 1) * P]).then_inc(ctx_in[p], 16)

            def load_first(w):
                sp.dma_start(stage0[:, w, :], w0[0, w, :, :]).then_inc(w_in[w], 16)

            def load_rows(b):
                sp.dma_start(xr[:, b, :], x[b, :, :]).then_inc(x_in[b], 16)

            load_first(1)
            load_context(0)
            load_rows(0)
            load_rows(1)
            sp.dma_start(lnw_bc, lnw.to_broadcast([P, D])).then_inc(lnw_in, 16)
            load_first(2)
            load_first(0)
            load_rows(2)
            load_rows(3)
            load_context(1)
            load_rows(4)
            load_rows(5)
            sp.dma_start(eq[:, 0:B * P // 4].bitcast(i32), mask).then_inc(mask_in, 16)
            for n in range(2):
                sp.dma_start(bias_sb[:, n, :], bias0[n, :, :]).then_inc(bias_in[n], 16)
            load_rows(6)
            load_rows(7)
            load_context(2)
            load_first(3)
            load_context(3)
            sp.dma_start(qw[:, :, :], qweight[:, 0:LO_BITS, :]).then_inc(quant_in, 16)
            sp.dma_start(lut[:, :, :], lut4).then_inc(quant_in, 16)
            sp.dma_start(fbias[:, :], ffn0_bias.to_broadcast([P, D])).then_inc(fbias_in, 16)
            sp.dma_start(qk_w[:, :], qk_norm).then_inc(qk_in, 16)

            def load_group(n):
                for w in range(4):
                    sp.wait_ge(w_lo_done[w], n + 1)
                    sp.dma_start(stage0[:, w, :], w0[n + 1, w, :, :]).then_inc(w_in[w], 16)

            def load_bias(n, parity):
                sp.wait_ge(bm_done, 4 * (n + 1))
                sp.dma_start(bias_sb[:, parity, :], bias0[n + 2, :, :]).then_inc(bias_in[parity], 16)

            with sp.Fori(0, NG // 2 - 1) as t:
                for parity in range(2):
                    load_group(2 * t + parity)
                    load_bias(2 * t + parity, parity)
            load_group(NG - 2)

            for piece, used, count in ((0, q_ps, U - 4), (1, k_ps, U - 4), (2, v_ps, U - 4), (3, y_ps, U - 4), (4, q_ps, U)):
                sp.wait_ge(used, count)
                sp.dma_start(plain1[:, 1024 * piece:1024 * (piece + 1)], w1[0, piece, :, :]).then_inc(first_in, 16)

            def load1(n, piece):
                sp.dma_start(stage1[:, piece % 2, :], w1[n, piece, :, :]).then_inc(w1_in[piece], 16)

            sp.wait_ge(acc_done, U)
            load1(1, 0)
            load1(1, 1)
            with sp.If(some_high(sp)):
                sp.dma_start(qw8[:, :, :], qweight).then_inc(hi_in, 16)
                sp.dma_start(lut8_sb[:, :, :], lut8).then_inc(hi_in, 16)
            for piece in range(2, 5):
                sp.wait_ge(w1_lo_done[piece - 2], 1)
                load1(1, piece)
            with sp.Fori(2, KV) as n:
                for piece, before, count in ((0, 4, n - 1), (1, 3, n - 1), (2, 0, n), (3, 1, n), (4, 2, n)):
                    sp.wait_ge(w1_lo_done[before], count)
                    load1(n, piece)

            sp.wait_ge(w1_lo_done[4], KV - 1)
            sp.wait_ge(w1_lo_done[3], KV - 1)
            sp.dma_start(stage1[:, :, :].bitcast(fp16)[:, 0, :], ffn1_w).then_inc(fw_in, 16)
            sp.dma_start(fbias16, ffn1_bias.to_broadcast([P, D])).then_inc(fbias_in, 16)
            for b in range(B):
                sp.wait_ge(facc_done, B + b + 1)
                sp.dma_start(out[b, :, :], xr[:, b, :]).then_inc(out_done, 16)
            sp.wait_ge(out_done, 16 * B)

        @block.gpsimd
        def _(pool):
            pool.memset(ident[:, :], 0.0).then_inc(ident_done, 1)
            pool.memset(half[:, :], -0.5).then_inc(half_done, 1)
            pool.wait_ge(ident_done, 1)
            pool.affine_select(out=ident[:, :], in_=ident[:, :], compare_op=ALU.not_equal, fill=1.0, base=0,
                               pattern=[[-1, P]], channel_multiplier=1).then_inc(ident_done, 1)
            pool.iota(shifts[:, :], pattern=[[1, 32]], base=0, channel_multiplier=0).then_inc(const_done, 1)

            def rsqrt(dst, src, exponent, ready, count, done):
                pool.wait_ge(ready, count)
                pool.tensor_tensor(dst, src, exponent, ALU.pow).then_inc(done, 1)

            def row_roots(phase_no, p):
                both, tiles = (2 if phase_no == 0 else 1), PARTS[phase_no][p]
                n = both * (tiles.stop - tiles.start)
                rsqrt(roots[:, 0:both, tiles], ve[:, 0:both, tiles], half[:, 0:n].rearrange("p (a n) -> p a n", a=both),
                      ve_done, 4 * phase_no + p + 1, rstd_done)

            def add_bias(phase_no, b, row):
                pool.wait_ge(z_done, B * (phase_no - 1) + b + 1)
                pool.tensor_tensor(xr[:, b, :], xr[:, b, :], row, ALU.add).then_inc(biased, 1)

            pool.wait_ge(half_done, 1)
            for p in range(3):
                row_roots(0, p)
            pool.wait_ge(negm_done, 1)

            def slot(t, j, tail=False):
                i, n, p, parity = BODY * t + j, 2 * t + j // 4, j % 4, (j // 4) % 2
                first = isinstance(t, int) and t == 0
                last = isinstance(t, int) and t == TL - 1
                if not tail:
                    if p == 0:
                        pool.wait_ge(bias_in[parity], 16 * (t + 1))
                    wait(pool, added, i - 1)
                    pool.tensor_tensor(
                        by4(bm[:, i % 2 if isinstance(t, int) else j % 2, :]).rearrange("p (h b) k -> p h b k", h=2),
                        by2(bias_sb[:, parity, :]).unsqueeze(2).to_broadcast([P, 2, 2, P]),
                        negm[:, 2 * p:2 * p + 2, :].unsqueeze(1).to_broadcast([P, 2, 2, P]),
                        ALU.add).then_inc(bm_done, 1)
                if not (first and j == 0):
                    pool.wait_ge(rn_done, i)
                    pool.tensor_tensor(by4(pr), by4(pr), rn[:, :].unsqueeze(2).to_broadcast([P, 4, P]),
                                       ALU.mult).then_inc(norm_done, 1)
                if first and j == 1:
                    row_roots(0, 3)
                if first and 2 <= j < 2 + B // 2:
                    pool.wait_ge(base_ready, 2)
                    for b in (2 * j - 4, 2 * j - 3):
                        pool.tensor_scalar(xr[:, b, :], xr[:, b, :], base_s[:, b:b + 1], base_b[:, b:b + 1],
                                           ALU.mult, ALU.add).then_inc(base_done, 1)
                if last and not tail and j == BODY - 1:
                    row_roots(1, 0)

            for j in range(BODY):
                slot(0, j)
            with pool.Fori(1, TL - 1) as t:
                for j in range(BODY):
                    slot(t, j)
            for j in range(BODY):
                slot(TL - 1, j)
            slot(TL - 1, BODY, tail=True)

            def first_low(k):
                piece = FIRST_ORDER[k]
                cols = slice(1024 * piece, 1024 * (piece + 1))
                pool.wait_ge(first_hi, k + 1)
                pool.tensor_tensor(w1_lo[:, 0, cols], plain1[:, cols], w1_hi[:, 0, cols].bitcast(fp32),
                                   ALU.subtract).then_inc(first_lo, 1)

            first_low(0)
            first_low(1)
            row_roots(1, 1)
            add_bias(1, 0, fbias[:, :])
            add_bias(1, 1, fbias[:, :])
            row_roots(1, 2)
            add_bias(1, 2, fbias[:, :])
            add_bias(1, 3, fbias[:, :])
            row_roots(1, 3)
            add_bias(1, 4, fbias[:, :])
            add_bias(1, 5, fbias[:, :])
            pool.wait_ge(any_done, 1)
            pool.partition_all_reduce(any_hi[:, 1:2], any_hi[:, 0:1], P, bass.bass_isa.ReduceOp.max).then_inc(all_done, 1)
            first_low(2)
            add_bias(1, 6, fbias[:, :])
            add_bias(1, 7, fbias[:, :])
            first_low(3)
            row_roots(2, 0)
            first_low(4)
            row_roots(2, 1)
            row_roots(2, 2)
            row_roots(2, 3)

            def k_root(count):
                rsqrt(k_r[:, :], k_ms[:, :], half[:, 0:2], k1_mean_done, count, k1_root_done)

            def q_root(count, parity):
                rsqrt(q_r[:, parity, :], q_ms[:, :], half[:, 0:4], q1_mean_done, count, q1_root_done)

            k_root(1)
            q_root(1, 0)

            def slot1(t, j, tail=False):
                i = BODY * t + j
                first = isinstance(t, int) and t == 0
                last = isinstance(t, int) and t == TL - 1
                if not (first and j == 0):
                    pool.wait_ge(recip1_done, i)
                    for half_p, done in ((0, norm1_first), (2, norm1_second)):
                        pool.tensor_tensor(p1[:, half_p:half_p + 2, :], p1[:, half_p:half_p + 2, :],
                                           rn1[:, half_p:half_p + 2].unsqueeze(2).to_broadcast([P, 2, 256]),
                                           ALU.mult).then_inc(done, 1)
                if not tail and not (last and j == BODY - 1):
                    k_root(i + 2)
                    q_root(i + 2, (j + 1) % 2)
                if last and not tail:
                    if j in (5, 7):
                        for b in (j - 5, j - 4):
                            add_bias(3, b, fbias1)
                    if j in (3, 5, 7):
                        row_roots(3, (j - 3) // 2)

            for j in range(BODY):
                slot1(0, j)
            with pool.Fori(1, TL - 1) as t:
                for j in range(BODY):
                    slot1(t, j)
            for j in range(BODY):
                slot1(TL - 1, j)
            slot1(TL - 1, BODY, tail=True)
            row_roots(3, 3)
            add_bias(3, 4, fbias1)
            add_bias(3, 5, fbias1)
            add_bias(3, 6, fbias1)
            row_roots(3, 4)
            add_bias(3, 7, fbias1)

        @block.scalar
        def _(act):
            act.wait_ge(gate_in, 16)
            nc.scalar.activation(tg[:, :], tg[:, :], ACT.Tanh).then_inc(tanh_done, 1)

            def transposed_hi(phase_no, b):
                act.wait_ge(xt_ps, B * phase_no + b + 1)
                nc.scalar.activation(xt_hi[:, :, tok(b)], by4(bank[XT_BANK[phase_no][b]][:, :]),
                                     ACT.Copy).then_inc(xt_hi_done, 1)

            def first_weight(w):
                act.wait_ge(w_in[w], 16)
                nc.scalar.activation(w0_hi[:, 0, w, :], stage0[:, w, :], ACT.Copy).then_inc(w_hi_done[w], 1)

            def context_hi(p):
                act.wait_ge(ctx_in[p], 16)
                nc.scalar.activation(ct_hi[:, :, 2 * p * P:2 * (p + 1) * P], ctx_raw[p], ACT.Copy).then_inc(ctx_hi_done, 1)

            def scaled_rows(b):
                act.wait_ge(z0_centred, b + 1)
                act.wait_ge(rstd_done, b // 2 + 1)
                nc.scalar.activation(z_rows(0, b), z_rows(0, b), ACT.Copy, scale=scale0[:, b:b + 1]).then_inc(z0_done, 1)

            first_weight(1)
            context_hi(0)
            first_weight(2)
            scaled_rows(0)
            scaled_rows(1)
            first_weight(0)
            transposed_hi(0, 0)
            transposed_hi(0, 1)
            scaled_rows(2)
            context_hi(1)
            scaled_rows(3)

            def exponentials(count):
                act.wait_ge(max_done, count)
                wait(act, pt_ps, count - 1)
                for a in range(4):
                    last_op = nc.scalar.activation(by4(pr)[:, a, :], by4(sc)[:, a, :], ACT.Exp,
                                                   bias=nmax[:, a:a + 1], accum_out=ssum[:, a:a + 1])
                last_op.then_inc(exp_done, 1)

            def output_hi(count, j):
                act.wait_ge(o_ps, count)
                wait(act, y_ps, count - 2)
                nc.scalar.activation(ot0_hi[:, j % 2, :], OB[:, :], ACT.Copy).then_inc(ot_hi_done, 1)

            def slot(t, j):
                i, n, p, parity = BODY * t + j, 2 * t + j // 4, j % 4, (j // 4) % 2
                first = isinstance(t, int) and t == 0
                last = isinstance(t, int) and t == TL - 1
                if not (first and j == 0):
                    exponentials(i)
                def next_weight(w):
                    act.wait_ge(w_in[w], 16 * (n + 2))
                    wait(act, (q_ps, k_ps, v_ps, y_ps)[w], 4 * n)
                    nc.scalar.activation(w0_hi[:, 1 - parity, w, :], stage0[:, w, :], ACT.Copy).then_inc(w_hi_done[w], 1)

                if first and j == 1:
                    transposed_hi(0, 4)
                    transposed_hi(0, 5)
                if not (last and j >= 4) and not (first and j == 0):
                    next_weight(p)
                act.wait_ge(q_ps, i + 1)
                wait(act, s_ps, i)
                nc.scalar.activation(qt, QB[:, :], ACT.Copy).then_inc(qt_done, 1)
                act.wait_ge(k_ps, i + 1)
                nc.scalar.activation(kt, KB[:, :], ACT.Copy).then_inc(kt_done, 1)
                if first and j == 1:
                    scaled_rows(6)
                    scaled_rows(7)
                act.wait_ge(v_ps, i + 1)
                wait(act, o_ps, i - 1)
                nc.scalar.activation(vs[:, j % 2, :], VB[:, :], ACT.Copy).then_inc(v_done, 1)
                if not (first and j == 0):
                    output_hi(i, j - 1)
                if first and j == 0:
                    transposed_hi(0, 2)
                    transposed_hi(0, 3)
                    scaled_rows(4)
                    scaled_rows(5)
                    context_hi(2)
                    first_weight(3)
                if first and j == 1:
                    next_weight(0)
                    transposed_hi(0, 6)
                    transposed_hi(0, 7)
                    context_hi(3)

            for j in range(BODY):
                slot(0, j)
            with act.Fori(1, TL - 1) as t:
                for j in range(BODY):
                    slot(t, j)
            for j in range(BODY):
                slot(TL - 1, j)

            def weight_hi(c):
                act.wait_ge(wlt_ps, c + 1)
                nc.scalar.activation(fw_hi[:, c, :], bank[WLT_BANK[c]][:, :], ACT.Copy).then_inc(fw_hi_done, 1)

            def first_rounded(k):
                piece = FIRST_ORDER[k]
                cols = slice(1024 * piece, 1024 * (piece + 1))
                act.wait_ge(first_in, 16 * 5)
                if k == 3:
                    act.wait_ge(wlt_ps, C)
                nc.scalar.activation(w1_hi[:, 0, cols], plain1[:, cols], ACT.Copy).then_inc(first_hi, 1)

            weight_hi(0)
            weight_hi(1)
            exponentials(U)
            weight_hi(2)
            weight_hi(3)
            transposed_hi(1, 0)
            transposed_hi(1, 1)
            first_rounded(0)
            first_rounded(1)
            output_hi(U, BODY - 1)
            first_rounded(2)
            first_rounded(3)
            first_rounded(4)
            for b in range(2, B):
                transposed_hi(1, b)
            with act.If(some_high(act)):
                for c in range(C):
                    act.wait_ge(hi_wt, c + 1)
                    nc.scalar.activation(fw8_hi[:, c, :], bank[4 + c][:, :], ACT.Copy).then_inc(hi_fw_hi, 1)
            transposed_hi(2, 0)
            transposed_hi(2, 1)

            def kv_out(count, place):
                act.wait_ge(kv1_ps, count)
                kv = by2(KVB[:, :])
                nc.scalar.activation(v_hi[:, place, :, :], kv[:, :, P:2 * P], ACT.Copy)
                for tile in range(2):
                    last_op = nc.scalar.activation(k_sq[:, tile, :], kv[:, tile, 0:P], ACT.Square,
                                                   accum_out=k_ss[:, tile:tile + 1])
                last_op.then_inc(k1_squared, 1)

            def q_out(count):
                act.wait_ge(q1_ps, count)
                nc.scalar.activation(q_sb[:, :], Q1B[:, :], ACT.Copy).then_inc(q1_copied, 1)
                nc.scalar.activation(q_sq[:, :], Q1B[:, :], ACT.Square).then_inc(q1_squared, 1)

            act.wait_ge(biased, B)
            kv_out(1, 0)
            q_out(1)

            def exponentials1(count, parity):
                act.wait_ge(shift1_done, count)
                wait(act, pt1_ps, count - 1)
                for a in range(4):
                    last_op = nc.scalar.activation(p1[:, a, :], by2((S0B, S1B)[a // 2][:, :])[:, a % 2, :], ACT.Exp,
                                                   bias=nb1[:, a:a + 1], scale=q_r[:, parity, a:a + 1],
                                                   accum_out=sum1[:, a:a + 1])
                last_op.then_inc(exp1_done, 1)

            def probabilities_hi(count):
                act.wait_ge(pt1_ps, count)
                wait(act, o1_ps, count - 1)
                for kc, done in ((0, pt1_hi_first), (1, pt1_hi_second)):
                    nc.scalar.activation(pt_hi[:, kc, :], (T0B, T1B)[kc][:, :], ACT.Copy).then_inc(done, 1)

            def output1_hi(count):
                act.wait_ge(o1_ps, count)
                wait(act, y1_ps, count - 1)
                nc.scalar.activation(ot1_hi[:, :], O1B[:, :], ACT.Copy).then_inc(ot1_hi_done, 1)

            def slot1(t, j):
                i = BODY * t + j
                first = isinstance(t, int) and t == 0
                last = isinstance(t, int) and t == TL - 1
                act.wait_ge(qt1_ps, i + 1)
                nc.scalar.activation(qt_hi[:, :], Q1B[:, :], ACT.Copy).then_inc(qt1_hi_done, 1)
                act.wait_ge(kt1_ps, i + 1)
                nc.scalar.activation(kt_hi[:, :], KVB[:, 0:256], ACT.Copy, scale=kw[:, 0:1]).then_inc(kt1_hi_done, 1)
                if first and j == 0:
                    for b in range(2, 6):
                        transposed_hi(2, b)
                if not (first and j == 0):
                    exponentials1(i, (j - 1) % 2)
                if first and j == 1:
                    transposed_hi(2, 6)
                    transposed_hi(2, 7)
                if not (last and j == BODY - 1):
                    wait(act, o1_ps, i - 2)
                    kv_out(i + 2, (j + 1) % 4)
                if last and j == BODY - 1:
                    transposed_hi(3, 0)
                if not (first and j == 0):
                    probabilities_hi(i)
                if not (last and j == BODY - 1):
                    q_out(i + 2)
                if not (first and j == 0):
                    output1_hi(i)
                if last and 3 <= j < 3 + C:
                    act.wait_ge(fw_in, 16)
                    act.wait_ge(y1_ps, U - BODY)
                    nc.scalar.activation(fw1[:, j - 3, :], by4(stage1[:, :, :].bitcast(fp16)[:, 0, :])[:, j - 3, :],
                                         ACT.Copy).then_inc(fw_hi_done, 1)

            for j in range(BODY):
                slot1(0, j)
            with act.Fori(1, TL - 1) as t:
                for j in range(BODY):
                    slot1(t, j)
            for j in range(BODY):
                slot1(TL - 1, j)
            transposed_hi(3, 1)
            exponentials1(U, (BODY - 1) % 2)
            transposed_hi(3, 2)
            transposed_hi(3, 3)
            probabilities_hi(U)
            transposed_hi(3, 4)
            output1_hi(U)
            for b in range(5, B):
                transposed_hi(3, b)

        @block.vector
        def _(dve):
            steps = [0]

            def link(op):
                steps[0] += 1
                op.then_inc(chain, 1)
                dve.wait_ge(chain, steps[0])

            def row_stats(phase_no, p):
                tiles = PARTS[phase_no][p]
                for b in range(tiles.start, tiles.stop):
                    if phase_no == 0:
                        dve.wait_ge(x_in[b], 16)
                    last_op = nc.vector.bn_stats(stats[:, b, :], xr[:, b, :])
                link(last_op)
                for b in range(tiles.start, tiles.stop):
                    last_op = nc.vector.bn_aggr(mv[:, b, :], stats[:, b, :])
                link(last_op)
                op = nc.vector.tensor_scalar(ve[:, 0, tiles], mv[:, tiles, 1], EPS_LN, None, ALU.add)
                if phase_no == 0:
                    link(op)
                    op = nc.vector.scalar_tensor_tensor(out=ve[:, 1, tiles], in0=ve[:, 0, tiles], scalar=EPS_RMS,
                                                        in1=mv[:, tiles, 1], op0=ALU.mult, op1=ALU.add)
                op.then_inc(ve_done, 1)

            def transposed_lo(phase_no, b):
                dve.wait_ge(xt_hi_done, B * phase_no + b + 1)
                nc.vector.tensor_tensor(xt_lo[:, :, tok(b)], by4(bank[XT_BANK[phase_no][b]][:, :]),
                                        xt_hi[:, :, tok(b)].bitcast(fp32), ALU.subtract).then_inc(xt_lo_done, 1)

            def normed_rows(phase_no, b):
                if phase_no == 0:
                    nc.vector.scalar_tensor_tensor(out=z_rows(0, b), in0=xr[:, b, :], scalar=mv[:, b, 0:1], in1=lnw_bc,
                                                   op0=ALU.subtract, op1=ALU.mult).then_inc(z0_centred, 1)
                    return
                part = [tiles.start <= b < tiles.stop for tiles in PARTS[phase_no]].index(True)
                dve.wait_ge(rstd_done, 4 * phase_no + part + 1)
                nc.vector.tensor_scalar(z_rows(phase_no, b), xr[:, b, :], mv[:, b, 0:1], rstd[:, b:b + 1],
                                        ALU.subtract, ALU.mult).then_inc(z_done, 1)

            def first_weight_lo(w):
                dve.wait_ge(w_hi_done[w], 1)
                nc.vector.tensor_tensor(w0_lo[:, 0, w, :], stage0[:, w, :], w0_hi[:, 0, w, :].bitcast(fp32),
                                        ALU.subtract).then_inc(w_lo_done[w], 1)

            def context_lo(p):
                pair = slice(2 * p * P, 2 * (p + 1) * P)
                dve.wait_ge(ctx_hi_done, p + 1)
                nc.vector.tensor_tensor(ct_lo[:, :, pair], ctx_raw[p], ct_hi[:, :, pair].bitcast(fp32),
                                        ALU.subtract).then_inc(ctx_lo_done, 1)

            first_weight_lo(1)
            context_lo(0)
            row_stats(0, 0)
            dve.wait_ge(lnw_in, 16)
            normed_rows(0, 0)
            normed_rows(0, 1)
            first_weight_lo(2)
            row_stats(0, 1)
            first_weight_lo(0)
            normed_rows(0, 2)
            transposed_lo(0, 0)
            transposed_lo(0, 1)
            normed_rows(0, 3)
            row_stats(0, 2)
            normed_rows(0, 4)
            context_lo(1)
            dve.wait_ge(mask_in, 16)
            by_batch = mask_raw.rearrange("p (b k) -> p b k", b=B)
            nc.vector.tensor_scalar(negm[:, :, :], by_batch, NEG, -NEG, ALU.mult, ALU.add).then_inc(negm_done, 1)
            transposed_lo(0, 2)
            normed_rows(0, 5)
            transposed_lo(0, 3)

            def residual_factors():
                dve.wait_ge(tanh_done, 1)
                dve.wait_ge(rstd_done, 4)
                link(nc.vector.tensor_tensor(base_b[:, :], mv[:, :, 0], rstd[:, :], ALU.mult))
                nc.vector.tensor_scalar(base_s[:, :], rstd[:, :], tg[:, 0:1], 1.0, ALU.mult, ALU.add).then_inc(base_ready, 1)
                link(nc.vector.tensor_scalar(base_b[:, :], base_b[:, :], -1.0, None, ALU.mult))
                nc.vector.tensor_scalar(base_b[:, :], base_b[:, :], tg[:, 0:1], None, ALU.mult).then_inc(base_ready, 1)

            def dequantising_constants():
                dve.wait_ge(fbias_in, 16)
                link(nc.vector.tensor_scalar(fbias[:, :], fbias[:, :], tg[:, 2:3], None, ALU.mult))
                dve.wait_ge(quant_in, 32)
                dve.wait_ge(const_done, 1)
                dve.wait_ge(qk_in, 16)
                nc.vector.tensor_copy(codes[:, :], shifts[:, 0:2 ** LO_BITS])
                nc.vector.tensor_tensor(kw[:, :], qk_w[:, 0:1], qk_w[:, 1:2], ALU.mult)
                link(nc.vector.memset(idx[:, :, :], 0))

            def unpack(plane, steps, packed=qw, scratch=unpacked, index=idx, link=link):
                words = packed[:, plane, :].unsqueeze(2).to_broadcast([P, C * D // 32, 32])
                bits = scratch.rearrange("p c (w s) -> p (c w) s", s=32)
                flat = scratch.rearrange("p c n -> p (c n)")
                codes8 = index[:, :, :].rearrange("p c n -> p (c n)")
                if "shift" in steps:
                    link(nc.vector.tensor_tensor(bits, words, shifts[:, :].unsqueeze(1).to_broadcast([P, C * D // 32, 32]),
                                                 ALU.logical_shift_right))
                if "mask" in steps:
                    link(nc.vector.tensor_scalar(flat, flat, 1, None, ALU.bitwise_and))
                if "add" in steps:
                    link(nc.vector.scalar_tensor_tensor(out=codes8, in0=flat, scalar=float(1 << plane), in1=codes8,
                                                        op0=ALU.mult, op1=ALU.add))

            UNPACK = {(2, "end"): (0, "shift"), (3, "middle"): (0, "mask"), (3, "end"): (0, "add"),
                      (4, "middle"): (1, "shift"), (4, "end"): (1, "mask"), (5, "middle"): (1, "add"),
                      (5, "end"): (2, "shift"), (6, "middle"): (2, "mask add"), (6, "end"): (3, "shift"),
                      (7, "middle"): (3, "mask"), (7, "end"): (3, "add")}

            def dequantise(code, c, count):
                wait(dve, wl_done, count - 1)
                nc.vector.tensor_scalar(eq[:, :], idx[:, c, :], codes[:, bass.ds(code, 1)],
                                        lut[:, c, bass.ds(code, 1)], ALU.is_equal, ALU.mult).then_inc(eq_done, 1)
                dve.wait_ge(eq_done, count)
                nc.vector.tensor_tensor(wl[:, c, :], wl[:, c, :], eq[:, :], ALU.add).then_inc(wl_done, 1)

            def maxima(count, parity):
                dve.wait_ge(s_ps, count)
                dve.wait_ge(bm_done, count)
                wait(dve, exp_done, count - 1)
                nc.vector.tensor_tensor(sc, SB[:, :], bm[:, parity, :], ALU.add).then_inc(added, 1)
                dve.wait_ge(added, count)
                nc.vector.tensor_reduce(nmax[:, :], by4(sc), axis=AX.X, op=ALU.max, negate=True).then_inc(max_done, 1)

            def accumulate(count, pair):
                dve.wait_ge(y_ps, count)
                nc.vector.scalar_tensor_tensor(out=xr[:, pair, :], in0=YA[:, :], scalar=tg[:, 0:1],
                                               in1=xr[:, pair, :], op0=ALU.mult, op1=ALU.add)
                nc.vector.scalar_tensor_tensor(out=xr[:, pair + 1, :], in0=YB[:, :], scalar=tg[:, 0:1],
                                               in1=xr[:, pair + 1, :], op0=ALU.mult, op1=ALU.add).then_inc(acc_done, 1)

            def inverse_sums(count, pair):
                dve.wait_ge(exp_done, count)
                nc.vector.reciprocal(rn[:, :], ssum[:, :]).then_inc(recip_done, 1)
                dve.wait_ge(recip_done, count)
                nc.vector.tensor_tensor(by2(rn[:, :]), by2(rn[:, :]),
                                        valid[:, pair:pair + 2].unsqueeze(1).to_broadcast([P, 2, 2]),
                                        ALU.mult).then_inc(rn_done, 1)

            def probabilities_out(count):
                dve.wait_ge(pt_ps, count)
                wait(dve, o_ps, count - 1)
                nc.vector.tensor_copy(ptr, TB[:, :]).then_inc(pt_done, 1)

            def output_lo(count, parity):
                dve.wait_ge(ot_hi_done, count)
                nc.vector.tensor_tensor(ot0_lo[:, parity, :], OB[:, :], ot0_hi[:, parity, :].bitcast(fp32),
                                        ALU.subtract).then_inc(ot_lo_done, 1)

            def slot(t, j):
                i, n, p, parity = BODY * t + j, 2 * t + j // 4, j % 4, (j // 4) % 2
                first = isinstance(t, int) and t == 0
                last = isinstance(t, int) and t == TL - 1
                lag1 = not (first and j < 1)

                def next_weight_lo(w):
                    dve.wait_ge(w_hi_done[w], n + 2)
                    if first and j < B // 2:
                        dve.wait_ge(ctx_lo_done, w + 1)
                    nc.vector.tensor_tensor(w0_lo[:, 1 - parity, w, :], stage0[:, w, :],
                                            w0_hi[:, 1 - parity, w, :].bitcast(fp32),
                                            ALU.subtract).then_inc(w_lo_done[w], 1)

                if lag1:
                    maxima(i, (j - 1) % 2)
                if not (first and j < 3):
                    if first and j < 3 + B // 2:
                        dve.wait_ge(base_done, 2 * (j - 3) + 2)
                    accumulate(i - 2, 2 * ((j - 3) % 4))
                if first and j == 1:
                    transposed_lo(0, 4)
                    transposed_lo(0, 5)
                    nc.vector.tensor_reduce(valid[:, :], by_batch, axis=AX.X, op=ALU.max).then_inc(valid_done, 1)
                    dve.wait_ge(valid_done, 1)
                if lag1:
                    inverse_sums(i, 2 * ((j - 1) % 4))
                if first and j == 1:
                    row_stats(0, 3)
                    probabilities_out(1)
                    normed_rows(0, 6)
                    normed_rows(0, 7)
                    context_lo(2)
                    first_weight_lo(3)
                if not (last and j >= 4) and not (first and j == 0):
                    next_weight_lo(p)
                if last and j == BODY - 1:
                    dve.wait_ge(acc_done, U - 3)
                    row_stats(1, 0)
                if first and j == 2:
                    residual_factors()
                    context_lo(3)
                if first and j == 3:
                    next_weight_lo(0)
                if first and (j, "middle") in UNPACK:
                    unpack(*UNPACK[j, "middle"])
                if lag1:
                    if not (first and j == 1):
                        probabilities_out(i)
                    output_lo(i, (j - 1) % 2)
                if first:
                    if j == 1:
                        transposed_lo(0, 6)
                        transposed_lo(0, 7)
                    elif j >= 2:
                        if j == 2:
                            dequantising_constants()
                        unpack(*UNPACK[j, "end"])
                    if j == BODY - 1:
                        link(nc.vector.memset(wl[:, :, :], 0.0))
                elif not last:
                    dequantise(2 * (t - 1) + j // 4, j % 4, BODY * (t - 1) + j + 1)
                else:
                    for k in range(2):
                        dequantise(2 * (TL - 2 + k) + j // 4, j % 4, BODY * (TL - 2) + 2 * j + k + 1)

            for j in range(BODY):
                slot(0, j)
            with dve.Fori(1, TL - 1) as t:
                for j in range(BODY):
                    slot(t, j)
            for j in range(BODY):
                slot(TL - 1, j)

            def weight_lo(c):
                dve.wait_ge(fw_hi_done, c + 1)
                nc.vector.tensor_tensor(fw_lo[:, c, :], bank[WLT_BANK[c]][:, :], fw_hi[:, c, :].bitcast(fp32),
                                        ALU.subtract).then_inc(fw_lo_done, 1)

            def feed_forward(phase_no, gate, b):
                count = B * (phase_no // 2) + b + 1
                dve.wait_ge(fy_ps, count)
                dve.wait_ge(biased, count)
                nc.vector.scalar_tensor_tensor(out=xr[:, b, :], in0=bank[FFN_BANK[phase_no][b]][:, :], scalar=gate, in1=xr[:, b, :],
                                               op0=ALU.mult, op1=ALU.add).then_inc(facc_done, 1)

            def token_gates(part):
                dve.wait_ge(rstd_done, 4 + part.stop // 2)
                link(nc.vector.tensor_tensor(norm_sq[:, part], mv[:, part, 1], rstd[:, part], ALU.mult))
                link(nc.vector.tensor_tensor(norm_sq[:, part], norm_sq[:, part], rstd[:, part], ALU.mult))
                link(nc.vector.tensor_scalar(gate_hi[:, part], norm_sq[:, part], float(D), EST_T ** 2, ALU.mult, ALU.is_gt))
                link(nc.vector.tensor_scalar(gate_lo[:, part], gate_hi[:, part], -1.0, 1.0, ALU.mult, ALU.add))
                if part.stop == B:
                    nc.vector.tensor_reduce(any_hi[:, 0:1], gate_hi[:, :], axis=AX.X, op=ALU.max).then_inc(any_done, 1)
                    dve.wait_ge(any_done, 1)
                    link(nc.vector.tensor_scalar(gate_hi[:, :], gate_hi[:, :], tg[:, 2:3], None, ALU.mult))
                link(nc.vector.tensor_scalar(gate_lo[:, part], gate_lo[:, part], tg[:, 2:3], None, ALU.mult))

            def low_forward(b):
                feed_forward(1, gate_lo[:, b:b + 1], b)

            maxima(U, (BODY - 1) % 2)
            weight_lo(0)
            normed_rows(1, 0)
            normed_rows(1, 1)
            weight_lo(1)
            inverse_sums(U, B - 2)
            accumulate(U - 2, 2)
            probabilities_out(U)
            weight_lo(2)
            transposed_lo(1, 0)
            weight_lo(3)
            output_lo(U, (BODY - 1) % 2)
            dve.wait_ge(acc_done, U - 2)
            row_stats(1, 1)
            accumulate(U - 1, 4)
            transposed_lo(1, 1)
            normed_rows(1, 2)
            normed_rows(1, 3)
            dve.wait_ge(acc_done, U - 1)
            row_stats(1, 2)
            token_gates(slice(0, 4))
            accumulate(U, 6)
            normed_rows(1, 4)
            normed_rows(1, 5)
            transposed_lo(1, 2)
            transposed_lo(1, 3)
            dve.wait_ge(acc_done, U)
            row_stats(1, 3)
            low_forward(0)
            token_gates(slice(4, B))
            transposed_lo(1, 4)
            low_forward(1)
            transposed_lo(1, 5)
            normed_rows(1, 6)
            normed_rows(1, 7)
            dve.wait_ge(all_done, 1)
            nc.vector.tensor_copy(flag[:, :], any_hi[:, 1:2]).then_inc(flag_done, 1)
            low_forward(2)
            transposed_lo(1, 6)
            transposed_lo(1, 7)
            low_forward(3)

            with dve.If(some_high(dve)):
                high_steps = [0]

                def high_link(op):
                    high_steps[0] += 1
                    op.then_inc(hi_chain, 1)
                    dve.wait_ge(hi_chain, high_steps[0])

                dve.wait_ge(hi_in, 32)
                dve.wait_ge(biased, B)
                dve.wait_ge(facc_done, 4)
                high_link(nc.vector.memset(idx8[:, :, :], 0))
                high_link(nc.vector.memset(code_now[:, :], 0.0))
                for plane in range(HI_BITS):
                    unpack(plane, "shift mask add", qw8, wl8[:, :, :].bitcast(i32), idx8, high_link)
                nc.vector.memset(wl8[:, :, :], 0.0).then_inc(hi_add, 1)
                first_code = high_steps[0]
                with dve.Fori(0, 2 ** HI_BITS) as code:
                    for c in range(C):
                        dve.wait_ge(hi_add, C * code + c + 1)
                        nc.vector.tensor_scalar(eq8[:, :], idx8[:, c, :], code_now[:, :], lut8_sb[:, c, bass.ds(code, 1)],
                                                ALU.is_equal, ALU.mult).then_inc(hi_eq, 1)
                        dve.wait_ge(hi_eq, C * code + c + 1)
                        nc.vector.tensor_tensor(wl8[:, c, :], wl8[:, c, :], eq8[:, :], ALU.add).then_inc(hi_add, 1)
                    nc.vector.tensor_scalar(code_now[:, :], code_now[:, :], 1.0, None, ALU.add).then_inc(hi_chain, 1)
                    dve.wait_ge(hi_chain, code + first_code + 1)
                for c in range(C):
                    dve.wait_ge(hi_fw_hi, c + 1)
                    nc.vector.tensor_tensor(fw8_lo[:, c, :], bank[4 + c][:, :], fw8_hi[:, c, :].bitcast(fp32),
                                            ALU.subtract).then_inc(hi_fw_lo, 1)
                for b in range(B):
                    dve.wait_ge(hi_y, b + 1)
                    nc.vector.scalar_tensor_tensor(out=xr[:, b, :], in0=bank[2 + b % 2][:, :], scalar=gate_hi[:, b:b + 1],
                                                   in1=xr[:, b, :], op0=ALU.mult, op1=ALU.add).then_inc(hi_acc, 1)
                dve.wait_ge(hi_acc, B)

            dve.wait_ge(facc_done, 2)
            row_stats(2, 0)
            low_forward(4)
            normed_rows(2, 0)
            normed_rows(2, 1)
            low_forward(5)
            dve.wait_ge(facc_done, 4)
            row_stats(2, 1)
            transposed_lo(2, 0)
            low_forward(6)
            transposed_lo(2, 1)
            normed_rows(2, 2)
            normed_rows(2, 3)
            low_forward(7)
            dve.wait_ge(facc_done, 6)
            row_stats(2, 2)
            dve.wait_ge(facc_done, B)
            row_stats(2, 3)

            def split_hi(n, piece, parity):
                dve.wait_ge(w1_in[piece], 16 * n)
                cols = slice(1024 * piece, 1024 * (piece + 1))
                nc.vector.tensor_scalar(w1_hi[:, parity, cols], stage1[:, piece % 2, :], 1.0, None,
                                        ALU.mult).then_inc(w1_hi_done[piece], 1)

            def split_lo(n, piece, parity):
                dve.wait_ge(w1_hi_done[piece], n)
                cols = slice(1024 * piece, 1024 * (piece + 1))
                nc.vector.tensor_tensor(w1_lo[:, parity, cols], stage1[:, piece % 2, :],
                                        w1_hi[:, parity, cols].bitcast(fp32), ALU.subtract).then_inc(w1_lo_done[piece], 1)

            def k_mean(count):
                dve.wait_ge(k1_squared, count)
                nc.vector.tensor_scalar(k_ms[:, :], k_ss[:, :], 1.0 / P, EPS_QK, ALU.mult, ALU.add).then_inc(k1_mean_done, 1)

            def v_low(count, place):
                dve.wait_ge(k1_squared, count)
                nc.vector.tensor_tensor(v_lo[:, place, :, :], by2(KVB[:, :])[:, :, P:2 * P],
                                        v_hi[:, place, :, :].bitcast(fp32), ALU.subtract).then_inc(v1_lo_done, 1)

            def k_scaled(count):
                dve.wait_ge(k1_root_done, count)
                for tile in range(2):
                    last_op = nc.vector.tensor_scalar(k_sb[:, tile, :], by2(KVB[:, :])[:, tile, 0:P],
                                                      k_r[:, tile:tile + 1], None, ALU.mult)
                last_op.then_inc(k1_scaled, 1)

            def q_mean(count):
                dve.wait_ge(q1_squared, count)
                nc.vector.tensor_reduce(q_ss[:, :], by4(q_sq[:, :]), axis=AX.X, op=ALU.add).then_inc(q1_sum_done, 1)
                dve.wait_ge(q1_sum_done, count)
                nc.vector.tensor_scalar(q_ms[:, :], q_ss[:, :], 1.0, EPS_QK * P, ALU.mult, ALU.add).then_inc(q1_mean_done, 1)

            v_low(1, 0)
            k_mean(1)
            normed_rows(2, 4)
            normed_rows(2, 5)
            k_scaled(1)
            q_mean(1)

            def maxima1(count, parity):
                dve.wait_ge(s1_ps, count)
                wait(dve, exp1_done, count - 1)
                for a in range(2):
                    last_op = nc.vector.tensor_reduce(nmax1[:, 2 * a:2 * a + 2], by2((S0B, S1B)[a][:, :]),
                                                      axis=AX.X, op=ALU.max, negate=True)
                last_op.then_inc(max1_done, 1)
                dve.wait_ge(max1_done, count)
                dve.wait_ge(q1_root_done, count)
                nc.vector.tensor_tensor(nb1[:, :], nmax1[:, :], q_r[:, parity, :], ALU.mult).then_inc(shift1_done, 1)

            def inverse_sums1(count):
                dve.wait_ge(exp1_done, count)
                nc.vector.reciprocal(rn1[:, :], sum1[:, :]).then_inc(recip1_done, 1)

            def accumulate1(count, b):
                dve.wait_ge(y1_ps, count)
                nc.vector.scalar_tensor_tensor(out=xr[:, b, :], in0=Y1B[:, :], scalar=tg[:, 1:2], in1=xr[:, b, :],
                                               op0=ALU.mult, op1=ALU.add).then_inc(acc1_done, 1)

            def probabilities_lo(count):
                for kc, ready in ((0, pt1_hi_first), (1, pt1_hi_second)):
                    dve.wait_ge(ready, count)
                    last_op = nc.vector.tensor_tensor(pt_lo[:, kc, :], (T0B, T1B)[kc][:, :],
                                                      pt_hi[:, kc, :].bitcast(fp32), ALU.subtract)
                last_op.then_inc(pt1_lo_done, 1)

            def output1_lo(count):
                dve.wait_ge(ot1_hi_done, count)
                nc.vector.tensor_tensor(ot1_lo[:, :], O1B[:, :], ot1_hi[:, :].bitcast(fp32),
                                        ALU.subtract).then_inc(ot1_lo_done, 1)

            def slot1(t, j):
                i = BODY * t + j
                first = isinstance(t, int) and t == 0
                last = isinstance(t, int) and t == TL - 1
                lag1 = not (first and j < 1)
                ahead = not (last and j == BODY - 1)
                if lag1:
                    maxima1(i, (j - 1) % 2)
                dve.wait_ge(qt1_hi_done, i + 1)
                nc.vector.tensor_tensor(qt_lo[:, :], Q1B[:, :], qt_hi[:, :].bitcast(fp32), ALU.subtract).then_inc(qt1_lo_done, 1)
                dve.wait_ge(kt1_hi_done, i + 1)
                nc.vector.scalar_tensor_tensor(out=kt_lo[:, :], in0=KVB[:, 0:256], scalar=kw[:, 0:1],
                                               in1=kt_hi[:, :].bitcast(fp32), op0=ALU.mult,
                                               op1=ALU.subtract).then_inc(kt1_lo_done, 1)
                if first and j == 0:
                    transposed_lo(2, 2)
                    transposed_lo(2, 3)
                    normed_rows(2, 6)
                    normed_rows(2, 7)
                if not last and 1 <= j < 6:
                    split_lo(t + 1, j - 1, (t + 1) % 2)
                if lag1:
                    inverse_sums1(i)
                if not (first and j < 2):
                    accumulate1(i - 1, (j - 2) % B)
                if last and j == BODY - 1:
                    transposed_lo(3, 0)
                    probabilities_lo(i)
                if last and j in (3, 5, 7):
                    dve.wait_ge(acc1_done, i - 1)
                    row_stats(3, (j - 3) // 2)
                if last and j == 2:
                    dve.wait_ge(fbias_in, 32)
                    nc.vector.tensor_scalar(fbias1, fbias16, tg[:, 3:4], None, ALU.mult)
                if last and j in (4, 6):
                    normed_rows(3, j - 4)
                    normed_rows(3, j - 3)
                if ahead:
                    v_low(i + 2, (j + 1) % 4)
                    k_mean(i + 2)
                if first and j == 0:
                    transposed_lo(2, 4)
                    transposed_lo(2, 5)
                if first and j == 1:
                    transposed_lo(2, 6)
                    transposed_lo(2, 7)
                if not last and j < 5:
                    wait(dve, y1_ps if j >= 3 else q1_ps, 8 * t)
                    split_hi(t + 1, j, (t + 1) % 2)
                if lag1 and not (last and j == BODY - 1):
                    probabilities_lo(i)
                if ahead:
                    k_scaled(i + 2)
                    q_mean(i + 2)
                if lag1:
                    output1_lo(i)
            for j in range(BODY):
                slot1(0, j)
            with dve.Fori(1, TL - 1) as t:
                for j in range(BODY):
                    slot1(t, j)
            for j in range(BODY):
                slot1(TL - 1, j)

            last_gate = tg[:, 3:4]
            maxima1(U, (BODY - 1) % 2)
            feed_forward(3, last_gate, 0)
            transposed_lo(3, 1)
            normed_rows(3, 4)
            normed_rows(3, 5)
            inverse_sums1(U)
            accumulate1(U - 1, 6)
            dve.wait_ge(acc1_done, U - 1)
            row_stats(3, 3)
            transposed_lo(3, 2)
            transposed_lo(3, 3)
            normed_rows(3, 6)
            probabilities_lo(U)
            feed_forward(3, last_gate, 1)
            output1_lo(U)
            transposed_lo(3, 4)
            feed_forward(3, last_gate, 2)
            feed_forward(3, last_gate, 3)
            transposed_lo(3, 5)
            accumulate1(U, 7)
            dve.wait_ge(acc1_done, U)
            row_stats(3, 4)
            transposed_lo(3, 6)
            normed_rows(3, 7)
            feed_forward(3, last_gate, 4)
            feed_forward(3, last_gate, 5)
            transposed_lo(3, 7)
            feed_forward(3, last_gate, 6)
            feed_forward(3, last_gate, 7)

        @block.tensor
        def _(pe):
            def passes(out_ap, terms):
                n = len(terms)
                for c, (l_hi, l_lo, r_hi, r_lo) in enumerate(terms):
                    nc.tensor.matmul(out_ap, l_hi, r_hi, start=(c == 0), stop=False)
                    nc.tensor.matmul(out_ap, l_hi, r_lo, start=False, stop=False)
                    op = nc.tensor.matmul(out_ap, l_lo, r_hi, start=False, stop=(c == n - 1))
                return op

            def transpose_rows(phase_no, b):
                count = B * phase_no + b + 1
                pe.wait_ge(*((z0_done, count) if phase_no == 0 else (z_done, count - B)))
                if phase_no in (0, 2):
                    wait(pe, xt_lo_done, count - 4 if b >= 4 else 0)
                elif b >= 3 or (phase_no, b) == (3, 1):
                    pe.wait_ge(xt_lo_done, count - (1 if b == 1 else 2))
                place = z_rows(phase_no, b)
                for c in range(C):
                    op = nc.tensor.transpose(bank[XT_BANK[phase_no][b]][:, tok(c)], place[:, tok(c)], ident[:, :])
                op.then_inc(xt_ps, 1)

            pe.wait_ge(ident_done, 2)

            def transposed_probabilities(count):
                pe.wait_ge(norm_done, count)
                wait(pe, pt_done, count - 1)
                for a in range(4):
                    op = nc.tensor.transpose(by4(TB[:, :])[:, a, :], by4(pr)[:, a, :], ident[:, :])
                op.then_inc(pt_ps, 1)

            def attention_output(count, parity):
                pe.wait_ge(pt_done, count)
                pe.wait_ge(v_done, count)
                wait(pe, ot_lo_done, count - 1)
                for h in range(2):
                    for bb in range(2):
                        a = 2 * h + bb
                        v = vs[:, parity, 256 * bb + P * h:256 * bb + P * (h + 1)]
                        op = nc.tensor.matmul(by4(OB[:, :])[:, a, :], v, by4(ptr)[:, a, :], start=True, stop=True)
                op.then_inc(o_ps, 1)

            def output_projection(count, k, n):
                if k % 4 == 0:
                    pe.wait_ge(w_lo_done[3], n + 1)
                pe.wait_ge(ot_lo_done, count)
                wait(pe, acc_done, count - 1)
                par = k // 4
                for bb, yb in ((0, YA), (1, YB)):
                    op = passes(yb[:, :], [
                        (by4(ot0_hi[:, k % 2, :])[:, 2 * h + bb, :], by4(ot0_lo[:, k % 2, :])[:, 2 * h + bb, :],
                         w0_hi[:, par, 3, 512 * h:512 * (h + 1)], w0_lo[:, par, 3, 512 * h:512 * (h + 1)])
                        for h in range(2)])
                op.then_inc(y_ps, 1)

            def slot(t, j):
                i, n, p, parity = BODY * t + j, 2 * t + j // 4, j % 4, (j // 4) % 2
                first = isinstance(t, int) and t == 0
                wh, wlo = w0_hi[:, parity, :, :], w0_lo[:, parity, :, :]

                def projected(dst, w, xh, xl, done, free):
                    if p == 0:
                        pe.wait_ge(w_lo_done[w], n + 1)
                    if first and p == j:
                        pe.wait_ge(*((xt_lo_done, 2 * j + 2) if w == 0 else (ctx_lo_done, j + 1)))
                    wait(pe, free, i)
                    tokens = slice(2 * p * P, 2 * (p + 1) * P)
                    for h in range(2):
                        cols = lambda a, c: a[:, w, 256 * c + P * h:256 * c + P * (h + 1)]
                        op = passes(by2(dst[:, :])[:, h, :],
                                    [(cols(wh, c), cols(wlo, c), xh[:, c, tokens], xl[:, c, tokens]) for c in range(C)])
                    op.then_inc(done, 1)

                def values():
                    if p == 0:
                        pe.wait_ge(w_lo_done[2], n + 1)
                    wait(pe, v_done, i)
                    for bb in range(2):
                        b = 2 * p + bb
                        op = passes(by2(VB[:, :])[:, bb, :],
                                    [(ct_hi[:, c, tok(b)], ct_lo[:, c, tok(b)], wh[:, 2, 256 * c:256 * (c + 1)],
                                      wlo[:, 2, 256 * c:256 * (c + 1)]) for c in range(C)])
                    op.then_inc(v_ps, 1)

                if first and j == 0:
                    projected(KB, 1, ct_hi, ct_lo, k_ps, kt_done)
                    transpose_rows(0, 0)
                    transpose_rows(0, 1)
                    values()
                    projected(QB, 0, xt_hi, xt_lo, q_ps, qt_done)
                    transpose_rows(0, 2)
                    transpose_rows(0, 3)
                else:
                    projected(QB, 0, xt_hi, xt_lo, q_ps, qt_done)
                    if first and j == 1:
                        transpose_rows(0, 4)
                        transpose_rows(0, 5)
                    projected(KB, 1, ct_hi, ct_lo, k_ps, kt_done)
                    if first and j == 1:
                        pe.wait_ge(xt_lo_done, 6)
                    transposed_probabilities(i)
                    values()
                    attention_output(i, (j - 1) % 2)
                if not (first and j < 2):
                    if first and j == 2:
                        pe.wait_ge(xt_lo_done, B)
                    output_projection(i - 1, (j - 2) % BODY, 2 * t + (j - 2) // 4)
                if first and j == 1:
                    transpose_rows(0, 6)
                    transpose_rows(0, 7)
                pe.wait_ge(qt_done, i + 1)
                pe.wait_ge(kt_done, i + 1)
                wait(pe, added, i)
                for h in range(2):
                    for bb in range(2):
                        part = slice(256 * h + P * bb, 256 * h + P * (bb + 1))
                        op = nc.tensor.matmul(SB[:, part], qt[:, part], kt[:, part], start=True, stop=True)
                op.then_inc(s_ps, 1)

            for j in range(BODY):
                slot(0, j)
            with pe.Fori(1, TL - 1) as t:
                for j in range(BODY):
                    slot(t, j)
            for j in range(BODY):
                slot(TL - 1, j)

            def transpose_weight(c):
                if c < 3:
                    pe.wait_ge((qt_done, kt_done, v_done)[c], U)
                else:
                    pe.wait_ge(fw_lo_done, 1)
                for o in range(C):
                    op = nc.tensor.transpose(bank[WLT_BANK[c]][:, tok(o)], wl[:, o, tok(c)], ident[:, :])
                op.then_inc(wlt_ps, 1)

            def ffn(phase_no, b, terms):
                count = B * (phase_no // 2) + b + 1
                pe.wait_ge(xt_lo_done, B * phase_no + b + 1)
                if b >= 2:
                    pe.wait_ge(facc_done, count - 2)
                n = len(terms)
                for k, (x_part, w_part, c) in enumerate(terms):
                    op = nc.tensor.matmul(bank[FFN_BANK[phase_no][b]][:, :], x_part[:, c, tok(b)], w_part[:, c, :],
                                          start=(k == 0), stop=(k == n - 1))
                op.then_inc(fy_ps, 1)

            def low_ffn(b):
                ffn(1, b, [(x_part, w_part, c) for c in range(C)
                           for x_part, w_part in ((xt_hi, fw_hi), (xt_hi, fw_lo), (xt_lo, fw_hi))])

            def last_ffn(b):
                ffn(3, b, [(x_part, fw1, c) for c in range(C) for x_part in (xt_hi, xt_lo)])

            pe.wait_ge(wl_done, C * 2 ** LO_BITS)
            for c in range(C):
                transpose_weight(c)
            pe.wait_ge(added, U)
            transpose_rows(1, 0)
            pe.wait_ge(fw_lo_done, 2)
            transpose_rows(1, 1)
            transposed_probabilities(U)
            attention_output(U, (BODY - 1) % 2)
            output_projection(U - 1, BODY - 2, NG - 1)
            pe.wait_ge(fw_lo_done, C)
            low_ffn(0)
            output_projection(U, BODY - 1, NG - 1)
            transpose_rows(1, 2)
            transpose_rows(1, 3)
            low_ffn(1)
            transpose_rows(1, 4)
            transpose_rows(1, 5)
            low_ffn(2)
            transpose_rows(1, 6)
            transpose_rows(1, 7)
            low_ffn(3)
            with pe.If(some_high(pe)):
                pe.wait_ge(hi_add, C * 2 ** HI_BITS + 1)
                pe.wait_ge(acc_done, U)
                pe.wait_ge(ot_lo_done, U)
                for c in range(C):
                    for o in range(C):
                        op = nc.tensor.transpose(bank[4 + c][:, tok(o)], wl8[:, o, tok(c)], ident[:, :])
                    op.then_inc(hi_wt, 1)
                pe.wait_ge(hi_fw_lo, C)
                pe.wait_ge(facc_done, 4)
                pe.wait_ge(xt_lo_done, 2 * B)
                for b in range(B):
                    wait(pe, hi_acc, b - 1)
                    op = passes(bank[2 + b % 2][:, :], [(xt_hi[:, c, tok(b)], xt_lo[:, c, tok(b)], fw8_hi[:, c, :],
                                                         fw8_lo[:, c, :]) for c in range(C)])
                    op.then_inc(hi_y, 1)
                pe.wait_ge(hi_acc, B)
            low_ffn(4)
            low_ffn(5)
            transpose_rows(2, 0)
            low_ffn(6)
            transpose_rows(2, 1)
            low_ffn(7)
            def keys_values(b, parity, count):
                wait(pe, kt1_lo_done, count - 1)
                wait(pe, v1_lo_done, count - 1)
                for tile, (xh, xl) in enumerate(((ct_hi, ct_lo), (xt_hi, xt_lo))):
                    op = passes(by2(KVB[:, :])[:, tile, :],
                                [(xh[:, c, tok(b)], xl[:, c, tok(b)], w1_hi[:, parity, 256 * c:256 * (c + 1)],
                                  w1_lo[:, parity, 256 * c:256 * (c + 1)]) for c in range(C)])
                op.then_inc(kv1_ps, 1)

            def queries(b, parity, count):
                wait(pe, qt1_lo_done, count - 1)
                op = passes(Q1B[:, :], [(xt_hi[:, c, tok(b)], xt_lo[:, c, tok(b)],
                                         w1_hi[:, parity, 1024 + 512 * c:1024 + 512 * (c + 1)],
                                         w1_lo[:, parity, 1024 + 512 * c:1024 + 512 * (c + 1)]) for c in range(C)])
                op.then_inc(q1_ps, 1)

            pe.wait_ge(first_lo, 5)
            pe.wait_ge(xt_lo_done, 2 * B + 1)
            keys_values(0, 0, 1)
            queries(0, 0, 1)
            transpose_rows(2, 2)
            transpose_rows(2, 3)

            def output_projection1(count, par):
                pe.wait_ge(ot1_lo_done, count)
                wait(pe, acc1_done, count - 1)
                op = passes(Y1B[:, :], [(ot1_hi[:, tok(h)], ot1_lo[:, tok(h)],
                                         w1_hi[:, par, 3072 + 512 * h:3072 + 512 * (h + 1)],
                                         w1_lo[:, par, 3072 + 512 * h:3072 + 512 * (h + 1)]) for h in range(GQ)])
                op.then_inc(y1_ps, 1)

            def transposed_probabilities1(count):
                wait(pe, pt1_lo_done, count - 1)
                for half_p, ready in ((0, norm1_first), (2, norm1_second)):
                    pe.wait_ge(ready, count)
                    for a in range(half_p, half_p + 2):
                        for kc in range(2):
                            op = nc.tensor.transpose(by4((T0B, T1B)[kc][:, :])[:, a, :], p1[:, a, tok(kc)], ident[:, :])
                op.then_inc(pt1_ps, 1)

            def attention_output1(count, place):
                pe.wait_ge(pt1_lo_done, count)
                wait(pe, ot1_lo_done, count - 1)
                op = passes(O1B[:, :], [(v_hi[:, place, kc, :], v_lo[:, place, kc, :], pt_hi[:, kc, :], pt_lo[:, kc, :])
                                        for kc in range(2)])
                op.then_inc(o1_ps, 1)

            def slot1(t, j):
                i = BODY * t + j
                first = isinstance(t, int) and t == 0
                last = isinstance(t, int) and t == TL - 1
                ahead = not (last and j == BODY - 1)
                own, other = t % 2, (t + 1) % 2
                pe.wait_ge(q1_copied, i + 1)
                pe.wait_ge(q1_squared, i + 1)
                for a in range(4):
                    op = nc.tensor.transpose(by4(Q1B[:, :])[:, a, :], by4(q_sb[:, :])[:, a, :], ident[:, :])
                op.then_inc(qt1_ps, 1)
                pe.wait_ge(k1_scaled, i + 1)
                pe.wait_ge(v1_lo_done, i + 1)
                for a in range(2):
                    op = nc.tensor.transpose(KVB[:, tok(a)], k_sb[:, a, :], ident[:, :])
                op.then_inc(kt1_ps, 1)
                if not (first and j < 2):
                    output_projection1(i - 1, own if j >= 2 else other)
                if first and j < 2:
                    transpose_rows(2, 4 + 2 * j)
                    transpose_rows(2, 5 + 2 * j)
                if ahead:
                    if j == BODY - 1:
                        for piece in range(5):
                            pe.wait_ge(w1_lo_done[piece], t + 1)
                    if first:
                        pe.wait_ge(xt_lo_done, 2 * B + j + 2 if j < BODY - 1 else 3 * B)
                    keys_values((j + 1) % B, other if j == BODY - 1 else own, i + 2)
                if last and j == BODY - 1:
                    pe.wait_ge(kt1_lo_done, U)
                    transpose_rows(3, 0)
                if not (first and j < 1):
                    if first and j == 1:
                        pe.wait_ge(xt_lo_done, 3 * B - 2)
                    transposed_probabilities1(i)
                if ahead:
                    queries((j + 1) % B, other if j == BODY - 1 else own, i + 2)
                if last and j == BODY - 1:
                    pe.wait_ge(fw_hi_done, 2 * C)
                    pe.wait_ge(qt1_lo_done, U)
                    last_ffn(0)
                if not (first and j < 1):
                    if first and j == 1:
                        pe.wait_ge(xt_lo_done, 3 * B)
                    attention_output1(i, (j - 1) % 4)
                if last and j == BODY - 1:
                    transpose_rows(3, 1)
                if first and j == 0:
                    pe.wait_ge(facc_done, B)
                pe.wait_ge(qt1_lo_done, i + 1)
                pe.wait_ge(kt1_lo_done, i + 1)
                wait(pe, exp1_done, i)
                for a in range(4):
                    op = passes(by2((S0B, S1B)[a // 2][:, :])[:, a % 2, :],
                                [(qt_hi[:, tok(a)], qt_lo[:, tok(a)], kt_hi[:, :], kt_lo[:, :])])
                op.then_inc(s1_ps, 1)

            for j in range(BODY):
                slot1(0, j)
            with pe.Fori(1, TL - 1) as t:
                for j in range(BODY):
                    slot1(t, j)
            for j in range(BODY):
                slot1(TL - 1, j)

            output_projection1(U - 1, (KV - 1) % 2)
            pe.wait_ge(facc_done, B + 1)
            transpose_rows(3, 2)
            transpose_rows(3, 3)
            pe.wait_ge(exp1_done, U)
            last_ffn(1)
            transposed_probabilities1(U)
            last_ffn(2)
            transpose_rows(3, 4)
            attention_output1(U, (BODY - 1) % 4)
            last_ffn(3)
            transpose_rows(3, 5)
            output_projection1(U, (KV - 1) % 2)
            transpose_rows(3, 6)
            last_ffn(4)
            last_ffn(5)
            transpose_rows(3, 7)
            last_ffn(6)
            last_ffn(7)


def kernel(**inputs):
    import numpy as np
    import concourse.bacc as bacc
    from concourse.bass_utils import run_bass_kernel_spmd

    a = {k: np.asarray(v) for k, v in inputs.items()}

    def rows(w, groups):
        return w.reshape(C, P, groups, -1).transpose(2, 1, 0, 3)

    gates = np.concatenate([a["g_xattn"], a["g_ffn"]]).reshape(1, 4)
    qkv0 = [rows(a[f"L0_xattn_w_{n}"].T, NG).reshape(NG, P, 1024) for n in "qkv"]
    out0 = a["L0_xattn_w_out"].T.reshape(NG, 2, P, D).transpose(0, 2, 1, 3).reshape(NG, P, 1024)
    w0 = np.stack([*qkv0, out0], axis=1)
    kv1 = np.concatenate([rows(a["L1_xattn_Wk"], KV), rows(a["L1_xattn_Wv"], KV)], axis=3).reshape(KV, P, 1, 1024)
    q1 = rows(a["L1_xattn_Wq"], KV).reshape(KV, P, 2, 1024)
    o1 = a["L1_xattn_Wo"].reshape(KV, GQ, P, D).transpose(0, 2, 1, 3).reshape(KV, P, 2, 1024)
    w1 = np.concatenate([kv1, q1, o1], axis=2).transpose(0, 2, 1, 3)
    table = lambda t: t.reshape(C, P, -1).transpose(1, 0, 2)
    data = {
        "x": a["x"],
        "ctx_t": a["ctx_4096"].reshape(B * P, C, P).transpose(2, 1, 0),
        "mask": a["mask_BxSxS2_bk0"].view(np.uint8).transpose(1, 0, 2).copy().reshape(P, B * P).view(np.int32),
        "gates": gates,
        "w0": w0,
        "bias0": a["L0_xattn_position_bias"].reshape(NG, 2, P, P).transpose(0, 2, 1, 3).reshape(NG, P, 2 * P),
        "lnw": a["L0_xattn_ln_weight"].reshape(1, D),
        "qweight": a["L0_ffn_qweight"].reshape(HI_BITS, C, P, D // 32).transpose(2, 0, 1, 3).reshape(P, HI_BITS, C * D // 32),
        "lut4": table(a["L0_ffn_lut4"]),
        "lut8": table(a["L0_ffn_lut8"]),
        "ffn0_bias": a["L0_ffn_bias"].reshape(1, D),
        "w1": w1,
        "qk_norm": np.stack([a["L1_xattn_q_norm_w"], a["L1_xattn_k_norm_w"]], axis=1),
        "ffn1_w": a["L1_ffn_weight"].T.reshape(C, P, D).transpose(1, 0, 2).reshape(P, C * D),
        "ffn1_bias": a["L1_ffn_bias"].reshape(1, D),
    }
    data = {k: np.ascontiguousarray(v) for k, v in data.items()}
    nc = bacc.Bacc("TRN2", target_bir_lowering=False, num_devices=1)
    args = [nc.dram_tensor(k, v.shape, mybir.dt.from_np(v.dtype), kind="ExternalInput").ap() for k, v in data.items()]
    args.append(nc.dram_tensor("out", (B, P, D), fp32, kind="ExternalOutput").ap())
    build(nc, *args)
    r = run_bass_kernel_spmd(nc, [data], core_ids=[0])
    return r.results[0]["out"]
```
